# Optimizing a Trainium2 kernel written in Bass

```python
import numpy as np
import jax
import jax.numpy as jnp

def _softmax(x, axis=-1):
    return jax.nn.softmax(x, axis=axis)

def _gelu(x):
    return jax.nn.gelu(x, approximate=True)

def _silu(x):
    return jax.nn.silu(x)

def _sigmoid(x):
    return jax.nn.sigmoid(x)

def _layernorm(x, axis=-1, eps=1e-05):
    m = jnp.mean(x, axis=axis, keepdims=True)
    v = jnp.var(x, axis=axis, keepdims=True)
    return (x - m) / jnp.sqrt(v + eps)

def _scatter_add(tgt, idx, src, axis=0):
    return tgt.at[idx].add(src)

def _segment_sum(src, seg, n):
    return jax.ops.segment_sum(src, seg, n)
kernel_name = 'mk_decoder_preln_d2_seqx_r4_33302b'

def setup_inputs(seed: int=0):
    np.random.seed(seed)
    _w = jnp.asarray

    def _rec_inputs():
        import jax
        import jax.numpy as jnp
        _rk = jax.random.key(seed)
        x = -0.0002928 + 1 * jax.random.normal(jax.random.fold_in(_rk, 1), (8, 256, 256), jnp.float32)
        _lenS = 256 - jax.random.randint(jax.random.fold_in(_rk, 7), (8,), 0, max(1, 256 // 4) + 1, jnp.int32)
        _lenS2 = 256 - jax.random.randint(jax.random.fold_in(_rk, 8), (8,), 0, max(1, 256 // 4) + 1, jnp.int32)
        _ctx_1024P = jax.random.normal(jax.random.fold_in(_rk, 11), (8, 16, 256), jnp.float32)
        _ctx_1024c = jax.random.dirichlet(jax.random.fold_in(_rk, 511), 0.3 * jnp.ones((16,), jnp.float32), (8, 256))
        _ctx_1024t = jnp.einsum('bsk,bkd->bsd', _ctx_1024c, _ctx_1024P)
        _ctx_1024t = _ctx_1024t * jax.lax.rsqrt(jnp.mean(jnp.square(_ctx_1024t)) + 1e-12) * 0.953939
        ctx_1024 = -1.39393e-06 + 0.999914 * (_ctx_1024t + 0.3 * jax.random.normal(jax.random.fold_in(_rk, 611), (8, 256, 256), jnp.float32))
        return (x, ctx_1024)
    x, ctx_1024 = _rec_inputs()

    def _L0_attn_setup():
        import jax, jax.numpy as jnp
        import numpy as np
        B, N, C, H = (4, 2048, 256, 16)
        D = C // H
        EPS = 1e-05
        key = jax.random.key(seed)
        ks = jax.random.split(key, 10)
        s = 1.0 / np.sqrt(C)
        return {'x': jax.random.normal(ks[0], (B, N, C), jnp.float32), 'Wq': jax.random.uniform(ks[1], (C, C), jnp.float32, -s, s), 'bq': jax.random.uniform(ks[2], (C,), jnp.float32, -s, s), 'Wk': jax.random.uniform(ks[3], (C, C), jnp.float32, -s, s), 'bk': jax.random.uniform(ks[4], (C,), jnp.float32, -s, s), 'Wv': jax.random.uniform(ks[5], (C, C), jnp.float32, -s, s), 'bv': jax.random.uniform(ks[6], (C,), jnp.float32, -s, s), 'Wo': jax.random.uniform(ks[7], (C, C), jnp.float32, -s, s), 'bo': jax.random.uniform(ks[8], (C,), jnp.float32, -s, s), 'ln_g': jnp.ones((C,), jnp.float32), 'ln_b': jnp.zeros((C,), jnp.float32)}
    _L0_attn_all = _L0_attn_setup()
    _L0_attn_in = {k: v for k, v in _L0_attn_all.items() if k in ('Wq', 'bq', 'Wk', 'bk', 'Wv', 'bv', 'Wo', 'bo', 'ln_g', 'ln_b')}
    del _L0_attn_all

    def _L0_xattn_setup():
        import jax, jax.numpy as jnp
        import numpy as np
        NUM_HEADS = 16
        B, S, D = (2, 512, 256)
        key = jax.random.key(seed)
        ks = jax.random.split(key, 6)
        return {'q': jax.random.normal(ks[0], (B, S, D), dtype=jnp.float32), 'k': jax.random.normal(ks[1], (B, S, D), dtype=jnp.float32), 'v': jax.random.normal(ks[2], (B, S, D), dtype=jnp.float32), 'wq': jax.random.normal(ks[3], (D, D), dtype=jnp.float32) * (1.0 / np.sqrt(D)), 'wk': jax.random.normal(ks[4], (D, D), dtype=jnp.float32) * (1.0 / np.sqrt(D)), 'wv': jax.random.normal(ks[5], (D, D), dtype=jnp.float32) * (1.0 / np.sqrt(D))}
    _L0_xattn_all = _L0_xattn_setup()
    _L0_xattn_in = {k: v for k, v in _L0_xattn_all.items() if k in ('wq', 'wk', 'wv')}
    del _L0_xattn_all

    def _L0_ffn_setup():
        import jax, jax.numpy as jnp
        import numpy as np
        D_MODEL, D_FF, RANK = (256, 1024, 64)
        B, S = (4, 1024)
        key = jax.random.key(seed)
        ks = jax.random.split(key, 7)
        return {'x': jax.random.normal(ks[0], (B, S, D_MODEL), dtype=jnp.float32), 'U1': jax.random.normal(ks[1], (D_MODEL, RANK), dtype=jnp.float32) * 0.02, 'V1': jax.random.normal(ks[2], (RANK, D_FF), dtype=jnp.float32) * 0.02, 'b1': jnp.zeros((D_FF,), dtype=jnp.float32), 'U2': jax.random.normal(ks[3], (D_FF, RANK), dtype=jnp.float32) * 0.02, 'V2': jax.random.normal(ks[4], (RANK, D_MODEL), dtype=jnp.float32) * 0.02, 'b2': jnp.zeros((D_MODEL,), dtype=jnp.float32)}
    _L0_ffn_all = _L0_ffn_setup()
    _L0_ffn_in = {k: v for k, v in _L0_ffn_all.items() if k in ('U1', 'V1', 'b1', 'U2', 'V2', 'b2')}
    del _L0_ffn_all

    def _L1_attn_setup():
        import jax, jax.numpy as jnp
        import numpy as np
        B, S, D, K = (4, 1024, 256, 64)
        key = jax.random.key(seed)
        kx, kq, kk, kv, ko = jax.random.split(key, 5)
        scale = 1.0 / np.sqrt(D)
        return {'x': jax.random.normal(kx, (B, S, D), dtype=jnp.float32), 'Wq': jax.random.uniform(kq, (K, D), dtype=jnp.float32, minval=-scale, maxval=scale), 'Wk': jax.random.uniform(kk, (K, D), dtype=jnp.float32, minval=-scale, maxval=scale), 'Wv': jax.random.uniform(kv, (K, D), dtype=jnp.float32, minval=-scale, maxval=scale), 'Wo': jax.random.uniform(ko, (D, K), dtype=jnp.float32, minval=-1.0 / np.sqrt(K), maxval=1.0 / np.sqrt(K))}
    _L1_attn_all = _L1_attn_setup()
    _L1_attn_in = {k: v for k, v in _L1_attn_all.items() if k in ('Wq', 'Wk', 'Wv', 'Wo')}
    del _L1_attn_all

    def _L1_xattn_setup():
        import jax, jax.numpy as jnp
        import numpy as np
        B, S, E, NH = (1, 512, 256, 8)
        DH = E // NH
        EPS_BACKEND = 1e-06
        EPS_NORM = 1e-05
        key = jax.random.key(seed)
        ks = jax.random.split(key, 8)
        q = jax.random.normal(ks[0], (B, S, E), jnp.float32)
        k = jax.random.normal(ks[1], (B, S, E), jnp.float32)
        v = jax.random.normal(ks[2], (B, S, E), jnp.float32)
        igate_w = jax.random.normal(ks[3], (NH, 3 * E), jnp.float32) * 0.02
        igate_b = jax.random.normal(ks[4], (NH,), jnp.float32) * 0.1
        fgate_w = jax.random.normal(ks[5], (NH, 3 * E), jnp.float32) * 0.02
        fgate_b = jnp.linspace(3.0, 6.0, NH).astype(jnp.float32)
        norm_w = 1.0 + 0.1 * jax.random.normal(ks[6], (E,), jnp.float32)
        return dict(q=q, k=k, v=v, igate_w=igate_w, igate_b=igate_b, fgate_w=fgate_w, fgate_b=fgate_b, norm_w=norm_w)
    _L1_xattn_all = _L1_xattn_setup()
    _L1_xattn_in = {k: v for k, v in _L1_xattn_all.items() if k in ('igate_w', 'igate_b', 'fgate_w', 'fgate_b', 'norm_w')}
    del _L1_xattn_all

    def _L1_ffn_setup():
        import jax, jax.numpy as jnp
        import numpy as np
        B, S, D, E, F = (2, 256, 256, 14, 512)
        key = jax.random.key(seed)
        k0, k1, k2, k3 = jax.random.split(key, 4)
        h = jax.random.normal(k0, (B, S, D), jnp.float32)
        gate_w = jax.random.normal(k1, (E, D), jnp.float32) * 0.02
        w1 = jax.random.normal(k2, (E, D, F), jnp.float32) * (1.0 / np.sqrt(D).astype(np.float32))
        b1 = jnp.zeros((E, F), jnp.float32)
        w2 = jax.random.normal(k3, (E, F, D), jnp.float32) * (1.0 / np.sqrt(F).astype(np.float32))
        b2 = jnp.zeros((E, D), jnp.float32)
        return {'h': h, 'gate_w': gate_w, 'w1': w1, 'b1': b1, 'w2': w2, 'b2': b2}
    _L1_ffn_all = _L1_ffn_setup()
    _L1_ffn_in = {k: v for k, v in _L1_ffn_all.items() if k in ('gate_w', 'w1', 'b1', 'w2', 'b2')}
    del _L1_ffn_all
    return {'x': x, 'ctx_1024': ctx_1024, 'L0_attn_Wq': _L0_attn_in['Wq'], 'L0_attn_bq': _L0_attn_in['bq'], 'L0_attn_Wk': _L0_attn_in['Wk'], 'L0_attn_bk': _L0_attn_in['bk'], 'L0_attn_Wv': _L0_attn_in['Wv'], 'L0_attn_bv': _L0_attn_in['bv'], 'L0_attn_Wo': _L0_attn_in['Wo'], 'L0_attn_bo': _L0_attn_in['bo'], 'L0_attn_ln_g': _L0_attn_in['ln_g'], 'L0_attn_ln_b': _L0_attn_in['ln_b'], 'L0_xattn_wq': _L0_xattn_in['wq'], 'L0_xattn_wk': _L0_xattn_in['wk'], 'L0_xattn_wv': _L0_xattn_in['wv'], 'L0_ffn_U1': _L0_ffn_in['U1'], 'L0_ffn_V1': _L0_ffn_in['V1'], 'L0_ffn_b1': _L0_ffn_in['b1'], 'L0_ffn_U2': _L0_ffn_in['U2'], 'L0_ffn_V2': _L0_ffn_in['V2'], 'L0_ffn_b2': _L0_ffn_in['b2'], 'L1_attn_Wq': _L1_attn_in['Wq'], 'L1_attn_Wk': _L1_attn_in['Wk'], 'L1_attn_Wv': _L1_attn_in['Wv'], 'L1_attn_Wo': _L1_attn_in['Wo'], 'L1_xattn_igate_w': _L1_xattn_in['igate_w'], 'L1_xattn_igate_b': _L1_xattn_in['igate_b'], 'L1_xattn_fgate_w': _L1_xattn_in['fgate_w'], 'L1_xattn_fgate_b': _L1_xattn_in['fgate_b'], 'L1_xattn_norm_w': _L1_xattn_in['norm_w'], 'L1_ffn_gate_w': _L1_ffn_in['gate_w'], 'L1_ffn_w1': _L1_ffn_in['w1'], 'L1_ffn_b1': _L1_ffn_in['b1'], 'L1_ffn_w2': _L1_ffn_in['w2'], 'L1_ffn_b2': _L1_ffn_in['b2']}

def reference(x, ctx_1024, L0_attn_Wq, L0_attn_bq, L0_attn_Wk, L0_attn_bk, L0_attn_Wv, L0_attn_bv, L0_attn_Wo, L0_attn_bo, L0_attn_ln_g, L0_attn_ln_b, L0_xattn_wq, L0_xattn_wk, L0_xattn_wv, L0_ffn_U1, L0_ffn_V1, L0_ffn_b1, L0_ffn_U2, L0_ffn_V2, L0_ffn_b2, L1_attn_Wq, L1_attn_Wk, L1_attn_Wv, L1_attn_Wo, L1_xattn_igate_w, L1_xattn_igate_b, L1_xattn_fgate_w, L1_xattn_fgate_b, L1_xattn_norm_w, L1_ffn_gate_w, L1_ffn_w1, L1_ffn_b1, L1_ffn_w2, L1_ffn_b2):
    import jax
    import jax.numpy as jnp

    def _L0_attn_ref(x, Wq, bq, Wk, bk, Wv, bv, Wo, bo, ln_g, ln_b):
        import jax, jax.numpy as jnp
        import numpy as np
        B, N, C, H = (4, 2048, 256, 16)
        D = C // H
        EPS = 1e-05
        b, n, c = x.shape
        q = x @ Wq.T + bq
        k = x @ Wk.T + bk
        v = x @ Wv.T + bv
        split = lambda z: z.reshape(b, n, H, D).transpose(0, 2, 1, 3)
        q, k, v = (split(q), split(k), split(v))
        q = jax.nn.softmax(q, axis=-1)
        k = jax.nn.softmax(k, axis=-2)
        state = jnp.einsum('bhnd,bhne->bhde', k, v)
        out = jnp.einsum('bhnd,bhde->bhne', q, state)
        out = out.transpose(0, 2, 1, 3).reshape(b, n, c)
        mu = out.mean(-1, keepdims=True)
        var = out.var(-1, keepdims=True)
        out = (out - mu) * jax.lax.rsqrt(var + EPS) * ln_g + ln_b
        return out @ Wo.T + bo

    def _L0_xattn_ref(q, k, v, wq, wk, wv):
        import jax, jax.numpy as jnp
        import numpy as np
        NUM_HEADS = 16
        B, S, D = (2, 512, 256)
        b, s, d = q.shape
        h = NUM_HEADS
        hd = d // h

        def proj(x, w):
            return (x @ w.T).reshape(b, s, h, hd).transpose(0, 2, 1, 3)
        qh, kh, vh = (proj(q, wq), proj(k, wk), proj(v, wv))
        scale = 1.0 / jnp.sqrt(jnp.asarray(hd, q.dtype))
        scores = jnp.einsum('bhqd,bhkd->bhqk', qh, kh) * scale
        mask = jnp.tril(jnp.ones((s, s), dtype=bool))
        scores = jnp.where(mask, scores, jnp.asarray(0.0, scores.dtype))
        attn = jax.nn.softmax(scores, axis=-1)
        out = jnp.einsum('bhqk,bhkd->bhqd', attn, vh)
        return out.transpose(0, 2, 1, 3).reshape(b, s, d)

    def _L0_ffn_ref(x, U1, V1, b1, U2, V2, b2):
        import jax, jax.numpy as jnp
        import numpy as np
        D_MODEL, D_FF, RANK = (256, 1024, 64)
        B, S = (4, 1024)
        P = jnp.einsum('bsd,dr->bsr', x, U1)
        H = jax.nn.gelu(jnp.einsum('bsr,rf->bsf', P, V1) + b1)
        Q = jnp.einsum('bsf,fr->bsr', H, U2)
        return jnp.einsum('bsr,rd->bsd', Q, V2) + b2

    def _L1_attn_ref(x, Wq, Wk, Wv, Wo):
        import jax, jax.numpy as jnp
        import numpy as np
        B, S, D, K = (4, 1024, 256, 64)
        Q = jax.nn.elu(x @ Wq.T) + 1.0
        Kf = jax.nn.elu(x @ Wk.T) + 1.0
        V = x @ Wv.T
        KV_sum = jnp.cumsum(Kf[..., :, None] * V[..., None, :], axis=1)
        K_sum = jnp.cumsum(Kf, axis=1)
        num = jnp.einsum('bsk,bskm->bsm', Q, KV_sum)
        den = jnp.einsum('bsk,bsk->bs', Q, K_sum)[..., None]
        out = num / (den + 1e-06)
        return out @ Wo.T

    def _L1_xattn_ref(q, k, v, igate_w, igate_b, fgate_w, fgate_b, norm_w):
        import jax, jax.numpy as jnp
        import numpy as np
        B, S, E, NH = (1, 512, 256, 8)
        DH = E // NH
        EPS_BACKEND = 1e-06
        EPS_NORM = 1e-05
        Bq, Sq, Eq = q.shape
        nh = igate_w.shape[0]
        dh = Eq // nh
        gate_in = jnp.concatenate([q, k, v], axis=-1)
        ig = jnp.transpose(gate_in @ igate_w.T + igate_b, (0, 2, 1))
        fg = jnp.transpose(gate_in @ fgate_w.T + fgate_b, (0, 2, 1))
        qh = q.reshape(Bq, Sq, nh, dh).transpose(0, 2, 1, 3)
        kh = k.reshape(Bq, Sq, nh, dh).transpose(0, 2, 1, 3)
        vh = v.reshape(Bq, Sq, nh, dh).transpose(0, 2, 1, 3)
        log_f_cum = jnp.cumsum(jax.nn.log_sigmoid(fg), axis=-1)
        log_fg_mat = log_f_cum[:, :, :, None] - log_f_cum[:, :, None, :]
        ltr = jnp.tril(jnp.ones((Sq, Sq), dtype=bool))
        log_D = jnp.where(ltr, log_fg_mat + ig[:, :, None, :], -jnp.inf)
        max_log_D = jnp.max(log_D, axis=-1, keepdims=True)
        D = jnp.exp(log_D - max_log_D)
        qk = jnp.einsum('bhsd,bhtd->bhst', qh, kh) / jnp.sqrt(jnp.float32(dh))
        C = qk * D
        normalizer = jnp.maximum(jnp.abs(jnp.sum(C, axis=-1, keepdims=True)), jnp.exp(-max_log_D))
        h = jnp.einsum('bhst,bhtd->bhsd', C / (normalizer + EPS_BACKEND), vh)
        mean = jnp.mean(h, axis=-1, keepdims=True)
        var = jnp.var(h, axis=-1, keepdims=True)
        h_norm = (h - mean) / jnp.sqrt(var + EPS_NORM)
        h_norm = h_norm * norm_w.reshape(nh, dh)[None, :, None, :]
        return h_norm.transpose(0, 2, 1, 3).reshape(Bq, Sq, Eq)

    def _L1_ffn_ref(h, gate_w, w1, b1, w2, b2):
        import jax, jax.numpy as jnp
        import numpy as np
        B, S, D, E, F = (2, 256, 256, 14, 512)
        Bb, Ss, Dd = h.shape
        x = h.reshape(Bb * Ss, Dd)
        logits = x @ gate_w.T
        probs = jax.nn.softmax(logits, axis=-1)
        top2_p, top2_i = jax.lax.top_k(probs, 2)
        w = top2_p / jnp.maximum(top2_p.sum(-1, keepdims=True), 1e-10)
        hh = jnp.einsum('nd,edf->nef', x, w1) + b1
        hh = jax.nn.gelu(hh, approximate=False)
        all_out = jnp.einsum('nef,efd->ned', hh, w2) + b2
        n = jnp.arange(x.shape[0])
        out0 = all_out[n, top2_i[:, 0]]
        out1 = all_out[n, top2_i[:, 1]]
        moe_out = w[:, 0:1] * out0 + w[:, 1:2] * out1
        result = jnp.clip(x + moe_out, -100.0, 100.0).reshape(Bb, Ss, Dd)
        return result
    x = x + _L0_attn_ref(_layernorm(x, axis=-1), L0_attn_Wq, L0_attn_bq, L0_attn_Wk, L0_attn_bk, L0_attn_Wv, L0_attn_bv, L0_attn_Wo, L0_attn_bo, L0_attn_ln_g, L0_attn_ln_b)
    x = x + _L0_xattn_ref(_layernorm(x, axis=-1), ctx_1024, ctx_1024, L0_xattn_wq, L0_xattn_wk, L0_xattn_wv)
    x = x + _L0_ffn_ref(_layernorm(x, axis=-1), L0_ffn_U1, L0_ffn_V1, L0_ffn_b1, L0_ffn_U2, L0_ffn_V2, L0_ffn_b2)
    x = x + _L1_attn_ref(_layernorm(x, axis=-1), L1_attn_Wq, L1_attn_Wk, L1_attn_Wv, L1_attn_Wo)
    x = x + _L1_xattn_ref(_layernorm(x, axis=-1), ctx_1024, ctx_1024, L1_xattn_igate_w, L1_xattn_igate_b, L1_xattn_fgate_w, L1_xattn_fgate_b, L1_xattn_norm_w)
    x = x + _L1_ffn_ref(_layernorm(x, axis=-1), L1_ffn_gate_w, L1_ffn_w1, L1_ffn_b1, L1_ffn_w2, L1_ffn_b2)
    return x

_drawn_inputs = setup_inputs


def setup_inputs(seed=0):
    import zlib

    import numpy as np

    out = dict(_drawn_inputs(seed))
    spreads = {'L0_attn_ln_g': (1.0, 0.2),
     'L0_attn_ln_b': (0.0, 0.1),
     'L0_ffn_b1': (0.0, 0.697),
     'L0_ffn_b2': (0.0, 0.474),
     'L1_ffn_b1': (0.0, 1.453),
     'L1_ffn_b2': (0.0, 0.981)}
    factors = {'L0_attn_bq': 15.791,
     'L0_attn_bk': 64.0,
     'L0_ffn_U1': 8.0,
     'L0_ffn_V1': 8.0,
     'L0_ffn_U2': 5.329,
     'L0_ffn_V2': 5.389,
     'L1_attn_Wq': 64.0,
     'L1_attn_Wk': 64.0,
     'L1_xattn_igate_b': 64.0,
     'L1_xattn_fgate_w': 4.181,
     'L1_xattn_norm_w': 3.545}
    for name, (base, spread) in spreads.items():
        noise = np.random.default_rng([zlib.crc32(name.encode()), seed]).standard_normal(out[name].shape)
        drawn = base * np.exp(spread * noise) if base else spread * noise
        out[name] = jnp.asarray(drawn.astype(out[name].dtype))
    for name, factor in factors.items():
        out[name] = (out[name] * factor).astype(out[name].dtype)
    return out
```

```python
from contextlib import ExitStack

import numpy as np

import concourse.bass as bass
from concourse import mybir

F32 = mybir.dt.float32
BF16 = mybir.dt.bfloat16
I32 = mybir.dt.int32
U32 = mybir.dt.uint32
ALU = mybir.AluOpType
ACT = mybir.ActivationFunctionType
AX = mybir.AxisListType

P = 128
NB, S, D = 8, 256, 256
NT = S // P
TT = NB * NT
NC = D // P
LN_EPS = 1e-5
NEG = -3.0e38
WORK_WORDS = 34480
EARLY_WORDS = 12832
TURNED = ("L0_attn_Wq", "L0_attn_Wk", "L0_attn_Wv", "L0_attn_Wo", "L0_xattn_wv",
          "L1_attn_Wq", "L1_attn_Wk", "L1_attn_Wv", "L1_attn_Wo", "L1_xattn_igate_w", "L1_xattn_fgate_w",
          "L1_ffn_gate_w")
COLUMNS = ("L0_attn_bk", "L0_attn_ln_g", "L0_attn_ln_b", "L0_ffn_b1")


def wait(eng, sem, value):
    if not (isinstance(value, int) and value <= 0):
        eng.wait_ge(sem, value)


def over_batches(eng, phases, depth=None, n=NB, before_last=None):
    if depth is None:
        depth = max(lag for lag, _ in phases)
        depth += depth % 2
    for s in range(depth):
        for lag, phase in phases:
            if s >= lag:
                phase(s - lag, (s - lag) % 2)
    pairs = (n - depth) // 2
    with eng.Fori(0, pairs) as i:
        for u in range(2):
            for lag, phase in phases:
                phase(i * 2 + (depth + u - lag), (u - lag) % 2)
    most = max(lag for lag, _ in phases)
    final = min(k for k, (lag, _) in enumerate(phases) if lag == most)
    for s in range(depth + 2 * pairs, n + depth):
        for k, (lag, phase) in enumerate(phases):
            if s - lag == n - 1 and k == final and before_last is not None:
                before_last()
            if s - lag < n:
                phase(s - lag, (s - lag) % 2)


def wait_once(eng, b, sem, value):
    if isinstance(b, int) and b == 0:
        eng.wait_ge(sem, value)


def at_most(value, most):
    return min(value, most) if isinstance(value, int) else value


class Chain:

    def __init__(self, eng, sem, per):
        self.eng, self.sem, self.per = eng, sem, per

    def start(self, b):
        self.base, self.n = b * self.per, 0

    def mark(self, ins):
        self.n += 1
        ins.then_inc(self.sem, 1)
        return self.base + self.n

    def link(self, ins):
        self.eng.wait_ge(self.sem, self.mark(ins))

    def end(self):
        assert self.n == self.per, (self.n, self.per)


class Region:

    def __init__(self, c, name, words):
        self.space, self.words, self.used = c.sb(name, [P, words]), words, 0

    def clear(self):
        self.used = 0

    def take(self, shape, dt=F32):
        rows, *free = shape
        n = int(np.prod(free))
        words = n if dt != BF16 else (n + 1) // 2
        assert self.used + words <= self.words, ("SBUF", self.used + words)
        v = self.space[0:rows, self.used:self.used + words]
        self.used += words
        if dt != F32:
            v = v.bitcast(dt)
        if len(free) > 1:
            names = "abcdef"[:len(free)]
            v = v.rearrange(f"p ({' '.join(names)}) -> p {' '.join(names)}",
                            **{k: s for k, s in zip(names, free)})
        return v


class Core:

    def __init__(self, nc, ctx):
        self.nc, self.ctx = nc, ctx
        self.banks = [ctx.enter_context(nc.psum_tensor(f"bank{i}", [P, 512], F32)) for i in range(8)]
        self.work = Region(self, "work", WORK_WORDS)
        self.early = Region(self, "early", EARLY_WORDS)
        self.stage_sems, self.given = None, []
        self.next_norm = None

    def sb(self, name, shape, dt=F32):
        return self.ctx.enter_context(self.nc.sbuf_tensor(name, shape, dt))

    def sem(self, name):
        s = (self.stage_sems or self.ctx).enter_context(self.nc.semaphore(name))
        if self.stage_sems is not None:
            self.given.append(s)
        return s

    def lasting_sem(self, name):
        return self.ctx.enter_context(self.nc.semaphore(name))

    def alone(self, eng):
        eng.nop(nofuse=True)

    def new_stage(self):
        self.work.clear()

    def take(self, shape, dt=F32):
        return self.work.take(shape, dt)


def batch_of(x, b):
    return x[:, bass.ds(b * NT, NT)] if not isinstance(b, int) else x[:, b * NT:(b + 1) * NT]


def tile_of(x, b, t):
    return x[:, bass.ds(b * NT + t, 1)] if not isinstance(b, int) else x[:, b * NT + t:b * NT + t + 1]


class LayerNorm:

    def __init__(self, c, name, n_par=2):
        self.c = c
        self.stats = c.take([P, 2, NT, 6])
        self.mv = c.take([P, 2, NT, 2])
        self.var = c.take([P, 2, NT])
        self.rstd = c.take([P, 2, NT])
        self.xn = c.take([P, 2, NT, D])
        self.s_chain = c.sem(name + "_ln_chain")
        self.s_var = c.sem(name + "_ln_var")
        self.s_rstd = c.sem(name + "_ln_rstd")
        self.s_xn = c.sem(name + "_ln_xn")
        self.ahead = 0

    def vector_ahead(self, dve, x, parts):
        self.ahead, n = 0, self.ahead
        for k, phase in enumerate((self.statistics(dve, x), self.normalise(dve, x, None))):
            for b in range(n if k in parts else 0):
                phase(b, b % 2)
        self.ahead = n

    def gpsimd_ahead(self, pool):
        self.ahead, n = 0, self.ahead
        phase = self.gpsimd(pool)
        for b in range(n):
            phase(b, b % 2)
        self.ahead = n

    def is_done(self, b):
        return isinstance(b, int) and b < self.ahead

    def statistics(self, dve, x):
        ch = Chain(dve, self.s_chain, 2 * NT)

        def phase(b, par):
            if self.is_done(b):
                return
            ch.start(b)
            wait(dve, self.s_xn, b - 1)
            for t in range(NT):
                last = ch.mark(dve.bn_stats(self.stats[:, par, t, :], tile_of(x, b, t)))
            dve.wait_ge(self.s_chain, last)
            self.c.alone(dve)
            for t in range(NT):
                last = ch.mark(dve.bn_aggr(self.mv[:, par, t, :], self.stats[:, par, t, :]))
            ch.end()
            dve.wait_ge(self.s_chain, last)
            dve.tensor_scalar(self.var[:, par], self.mv[:, par, :, 1], LN_EPS, None, ALU.add).then_inc(self.s_var, 1)
        return phase

    def normalise(self, dve, x, s_turned):
        def phase(b, par):
            if self.is_done(b):
                return
            dve.wait_ge(self.s_rstd, b + 1)
            wait(dve, s_turned, b - 1)
            for t in range(NT):
                ins = dve.tensor_scalar(self.xn[:, par, t, :], tile_of(x, b, t), self.mv[:, par, t, 0:1],
                                        self.rstd[:, par, t:t + 1], ALU.subtract, ALU.mult)
            ins.then_inc(self.s_xn, 1)
        return phase

    def vector(self, dve, x, s_turned):
        first, second = self.statistics(dve, x), self.normalise(dve, x, s_turned)

        def phase(b, par):
            first(b, par)
            second(b, par)
        return phase

    def gpsimd(self, pool):
        def phase(b, par):
            if self.is_done(b):
                return
            pool.wait_ge(self.s_var, b + 1)
            pool.tensor_tensor(self.rstd[:, par], self.var[:, par], self.c.minus_half[:, 0:NT],
                               ALU.pow).then_inc(self.s_rstd, 1)
        return phase


def norm_ahead(c, eng, x, *free, parts=(0, 1)):
    def call():
        if c.next_norm is None:
            return
        for sem, value in free:
            eng.wait_ge(sem, value)
        if free:
            c.next_norm.vector_ahead(eng, x, parts)
        else:
            c.next_norm.gpsimd_ahead(eng)
    return call


def turn_over(pe, ident, src, bank, sem):
    for c in range(NC):
        for t in range(NT):
            ins = pe.transpose(bank[:, c * S + t * P:c * S + (t + 1) * P], src[:, t, c * P:(c + 1) * P],
                               ident[:, :])
    ins.then_inc(sem, 1)


class Weights:
    pass


def setup(c, x, w, ins):
    w.s_const = c.s_const = c.sem("constants")
    s_c = c.sem("constants_order")
    s_zero = c.sem("zeroed")
    w.s_x = [c.sem("x_first"), c.sem("x_second"), c.sem("x_rest")]

    def sb(name, shape):
        return c.early.take(shape)

    c.ident = c.sb("ident", [P, P])
    c.same_head = c.sb("same_head", [P, P])
    c.minus_half = c.sb("minus_half", [P, 16])
    c.ident_bf = c.sb("ident_bf", [P, P], BF16)
    c.causal = c.sb("causal", [P, 3 * P])
    c.masked = c.sb("masked", [P, 2, P], BF16)
    c.after = c.sb("after", [P, P])
    c.ones = c.sb("ones", [P, P])
    c.causal_T = c.sb("causal_T", [P, 3 * P])
    c.n_after = c.sb("n_after", [P, NT])
    c.i_minus_f, c.only_f = c.sb("i_minus_f", [P, 2, 64]), c.sb("only_f", [P, 2, 64])
    c.both_halves = c.sb("both_halves", [P, 64], BF16)
    w.gates = sb("gates", [P, 2 * NC, 184])
    w.gates_v = sb("gates_v", [P, NC, 2, 8])
    w.gate_b, w.norm_w = sb("gate_b", [P, 1]), sb("norm_w", [P, D])
    c.ctxT = c.early.take([P, NC, NB * S])
    w.u1, w.v1 = sb("u1", [P, NC, P]), sb("v1", [P, 1024])
    w.u2, w.v2 = sb("u2", [P, 8, 64]), sb("v2", [P, D])
    w.fb1, w.fb2 = sb("fb1", [P, 8]), sb("fb2", [P, D])
    w.lqk, w.lv, w.lo = sb("lqk", [P, NC, 2, P]), sb("lv", [P, NC, P]), sb("lo", [P, D + 2])
    w.cq, w.ck, w.cv = sb("cq", [P, NC, D]), sb("ck", [P, NC, D]), sb("cv", [P, NC, D])
    w.qv, w.bqv, w.k, w.bk, w.o = sb("qv", [P, NC, 2 * D]), sb("bqv", [P, 2 * D]), sb("k", [P, NC, D]), sb("bk", [P, NC]), sb("o", [P, NC, D])
    w.bo, w.ln_g, w.ln_b = sb("bo", [P, D]), sb("ln_g", [P, NC]), sb("ln_b", [P, NC])

    chunks = lambda a: a.rearrange("(n p) m -> p n m", p=P)
    loads = {
        "la": [(w.qv[:, :, 0:D], chunks(ins["L0_attn_WqT"])), (w.qv[:, :, D:2 * D], chunks(ins["L0_attn_WvT"])),
               (w.k[:, :, :], chunks(ins["L0_attn_WkT"])), (w.o[:, :, :], chunks(ins["L0_attn_WoT"])),
               (w.bqv[:, 0:D], ins["L0_attn_bq"].partition_broadcast(P)), (w.bqv[:, D:2 * D], ins["L0_attn_bv"].partition_broadcast(P)),
               (w.bo[:, :], ins["L0_attn_bo"].partition_broadcast(P)), (w.bk[:, :], (ins["L0_attn_bk"])),
               (w.ln_g[:, :], (ins["L0_attn_ln_g"])), (w.ln_b[:, :], (ins["L0_attn_ln_b"]))],
        "ca": [(w.cq[:, :, :], chunks(ins["L0_xattn_wq_h"])), (w.ck[:, :, :], chunks(ins["L0_xattn_wk_h"])),
               (w.cv[:, :, :], chunks(ins["L0_xattn_wvT"]))]
              + [(c.ctxT[:, n, :].rearrange("p (b s) -> p b s", b=NB),
                  ins["ctx_T"][:, n * P:(n + 1) * P, :].rearrange("b p s -> p b s")) for n in range(NC)],
        "lf": [(w.u1[:, :, 0:64], chunks(ins["L0_ffn_U1"])), (w.v1[0:64, :], ins["L0_ffn_V1"]),
               (w.u2[:, :, :], chunks(ins["L0_ffn_U2"])), (w.v2[0:64, :], ins["L0_ffn_V2"]),
               (w.v2[64:P, :], ins["L0_ffn_V2"]), (w.fb1[:, :], ins["L0_ffn_b1"]),
               (w.fb2[:, :], ins["L0_ffn_b2"].partition_broadcast(P))],
        "ga": [(w.gates[:, :, 56 + 64 * k:64 + 64 * k], chunks(ins[name][0:2 * D, :]))
               for k, name in enumerate(("L1_xattn_igate_wT", "L1_xattn_fgate_wT"))]
              + [(w.gates_v[:, :, k, :], chunks(ins[name][2 * D:3 * D, :]))
                 for k, name in enumerate(("L1_xattn_igate_wT", "L1_xattn_fgate_wT"))]
              + [(w.gate_b[:, :], ins["gate_b"]), (w.norm_w[:, :], ins["L1_xattn_norm_w"].partition_broadcast(P))],
        "cl": [(w.lqk[:, :, 0, 0:64], chunks(ins["L1_attn_WqT"])), (w.lqk[:, :, 1, 0:64], chunks(ins["L1_attn_WkT"])),
               (w.lv[:, :, 0:64], chunks(ins["L1_attn_WvT"])), (w.lo[0:64, 0:D], ins["L1_attn_WoT"])],
    }
    w.loaded = {k: (c.sem("w_" + k), 16 * len(v)) for k, v in loads.items()}

    def sync(sp):
        xv = ins["x"].rearrange("b (t p) d -> p (b t) d", p=P)
        sp.dma_start(x[:, 0:NT], xv[:, 0:NT]).then_inc(w.s_x[0], 16)
        for k in loads:
            if k == "lf":
                sp.wait_ge(s_zero, 7)
            for dst, src in loads[k]:
                sp.dma_start(dst, src).then_inc(w.loaded[k][0], 16)
            if k == "la":
                sp.dma_start(x[:, NT:2 * NT], xv[:, NT:2 * NT]).then_inc(w.s_x[1], 16)
                sp.dma_start(x[:, 2 * NT:], xv[:, 2 * NT:]).then_inc(w.s_x[2], 16)

    def vector(dve):
        for part in (w.u1[:, :, 64:P], w.v1[64:P, :], w.lqk[:, :, :, 64:P], w.lv[:, :, 64:P], w.lo[:, :],
                     w.gates[:, :, :]):
            ins = dve.memset(part, 0.0)
            ins.then_inc(s_zero, 1)
        dve.wait_ge(s_zero, 6)
        dve.memset(w.lo[64:65, D:D + 1], 1.0).then_inc(s_zero, 1)

    def gpsimd(pool):
        pool.memset(c.ident[:, :], 0.0).then_inc(s_c, 1)
        pool.memset(c.same_head[:, :], 1.0).then_inc(s_c, 1)
        pool.memset(c.minus_half[:, :], -0.5)
        pool.wait_ge(s_c, 2)
        pool.affine_select(out=c.ident[:, :], in_=c.ident[:, :], compare_op=ALU.not_equal, fill=1.0, base=0,
                           pattern=[[-1, P]], channel_multiplier=1).then_inc(s_i, 1)
        blocks = c.same_head[:, :].rearrange("p (h d) -> p h d", d=16)
        pool.affine_select(out=blocks, in_=blocks, compare_op=ALU.is_ge, fill=0.0, base=0,
                           pattern=[[-16, 8], [0, 16]], channel_multiplier=1).then_inc(s_c, 1)
        pool.wait_ge(s_c, 3)
        pool.affine_select(out=blocks, in_=blocks, compare_op=ALU.is_ge, fill=0.0, base=15,
                           pattern=[[16, 8], [0, 16]], channel_multiplier=-1).then_inc(w.s_const, 1)

    def later_constants(pool):
        pool.wait_ge(s_i, 1)
        pool.tensor_copy(c.ident_bf[:, :], c.ident[:, :])
        pool.memset(c.causal[:, :], 1.0).then_inc(s_i, 1)
        pool.memset(c.masked[:, :, :], 0.0).then_inc(s_i, 1)
        pool.memset(c.after[:, :], 0.0).then_inc(s_i, 1)
        pool.memset(c.ones[:, :], 1.0)
        pool.memset(c.causal_T[:, :], 1.0).then_inc(s_i, 1)
        for m in (c.i_minus_f[:, :, :], c.only_f[:, :, :], c.both_halves[:, :]):
            pool.memset(m, 0.0).then_inc(s_i, 1)
        pool.iota(n_after_i[:, :], pattern=[[-P, NT]], base=S - 1, channel_multiplier=-1).then_inc(s_i, 1)
        pool.wait_ge(s_i, 9)
        for m, fill, base in ((c.i_minus_f, 1.0, 0), (c.only_f, 1.0, -64)):
            pool.affine_select(out=m[:, :, :], in_=m[:, :, :], compare_op=ALU.not_equal, fill=fill, base=base,
                               pattern=[[0, 2], [-1, 64]], channel_multiplier=1).then_inc(s_i, 1)
        pool.affine_select(out=c.both_halves[:, :], in_=c.both_halves[:, :], compare_op=ALU.not_equal, fill=1.0,
                           base=0, pattern=[[-1, 64]], channel_multiplier=1).then_inc(s_i, 1)
        pool.wait_ge(s_i, 12)
        pool.affine_select(out=c.i_minus_f[:, :, :], in_=c.i_minus_f[:, :, :], compare_op=ALU.not_equal, fill=-1.0,
                           base=-64, pattern=[[0, 2], [-1, 64]], channel_multiplier=1)
        pool.affine_select(out=c.both_halves[:, :], in_=c.both_halves[:, :], compare_op=ALU.not_equal, fill=1.0,
                           base=-64, pattern=[[-1, 64]], channel_multiplier=1)
        for tile in (c.causal_T[:, 0:P], c.causal_T[:, 2 * P:3 * P]):
            pool.affine_select(out=tile, in_=tile, compare_op=ALU.is_ge, fill=0.0, base=0,
                               pattern=[[1, P]], channel_multiplier=-1)
        for tile in (c.causal[:, 0:P], c.causal[:, 2 * P:3 * P]):
            pool.affine_select(out=tile, in_=tile, compare_op=ALU.is_ge, fill=0.0, base=0,
                               pattern=[[-1, P]], channel_multiplier=1)
        pool.affine_select(out=c.masked[:, :, :], in_=c.masked[:, :, :], compare_op=ALU.is_ge, fill=-1e30, base=0,
                           pattern=[[0, 2], [1, P]], channel_multiplier=-1)
        pool.affine_select(out=c.after[:, :], in_=c.after[:, :], compare_op=ALU.is_ge, fill=1.0, base=0,
                           pattern=[[1, P]], channel_multiplier=-1)
        pool.tensor_copy(c.n_after[:, :], n_after_i[:, :]).then_inc(w.s_const, 1)

    n_after_i = c.sb("n_after_i", [P, NT], I32)
    s_i = c.sem("ident_order")
    c.later_constants = later_constants
    return {"sync": sync, "vector": vector, "gpsimd": gpsimd}


def wait_x(eng, w, b):
    eng.wait_ge(w.s_x[min(b, 2) if isinstance(b, int) else 2], 16)


def wait_weights(eng, w, key):
    eng.wait_ge(*w.loaded[key])


def linear_attention(c, x, w):
    H, HD = 16, 16
    banks, ident = c.banks, c.ident
    c.new_stage()
    ln = LayerNorm(c, "la")
    xnT = c.take([P, 2, NC, S])
    qv = c.take([P, 2, NT, 2 * D])
    kb = c.take([P, NC, S])
    nmax = c.take([P, NC])
    ek = c.take([P, 2, NC, S])
    ksum = c.take([P, 2, NC])
    rks = c.take([P, NC])
    qmax = c.take([P, NT * H])
    qs = c.take([P, NT, D])
    eq = c.take([P, 2, NT, D])
    qsum = c.take([P, NT * H])
    rq = c.take([P, NT * H])
    ekN = c.take([P, NT, D])
    eqT = c.take([P, NC, S])
    state = c.take([P, NC, P])
    o = c.take([P, NT, D])
    on = c.take([P, NT, D])
    onT = c.take([P, NC, S])
    o_stats, o_mv = c.take([P, NT, 6]), c.take([P, NT, 2])
    o_var, o_rstd = c.take([P, NT]), c.take([P, NT])

    b_turn = [banks[0], banks[1]]
    b_qv = [banks[2], banks[3]]
    b_k, b_state, b_out, b_y = banks[4], banks[5], banks[6], banks[7]

    sem = lambda n: c.sem("la_" + n)
    s_xT = sem("xT")
    s_xnT = sem("xnT")
    s_qv = sem("qv")
    s_k = sem("k")
    s_qv_sb = sem("qv_sb")
    s_kb = sem("kb")
    s_nmax = sem("nmax")
    s_qs = sem("qs")
    s_ek = sem("ek")
    s_eq = sem("eq")
    s_ekP = sem("ekP")
    s_eqP = sem("eqP")
    s_ekN = sem("ekN")
    s_eqT = sem("eqT")
    s_st = sem("st")
    s_state = sem("state")
    s_out = sem("out")
    s_osb = sem("osb")
    s_ovar = sem("ovar")
    s_orstd = sem("orstd")
    s_on = sem("on")
    s_onP = sem("onP")
    s_onT = sem("onT")
    s_y = sem("y")
    s_add = sem("add")
    s_bo = sem("bo")
    s_qsum, s_rq, s_rks = sem("qsum"), sem("rq"), sem("rks")
    s_qch, s_och = sem("q_chain"), sem("o_chain")

    def tensor(pe):
        pe.wait_ge(w.s_const, 1)

        def turn_x(b, par):
            pe.wait_ge(ln.s_xn, b + 1)
            wait(pe, s_eqT, b - 1)
            turn_over(pe, ident, ln.xn[:, par], b_turn[0], s_xT)

        def project(b, par):
            wait_once(pe, b, *w.loaded["la"])
            pe.wait_ge(s_xnT, b + 1)
            for t in range(NT):
                wait(pe, s_qv_sb, b * NT + t - 1)
                for n in range(NC):
                    ins = pe.matmul(b_qv[t][:, :], xnT[:, par, n, t * P:(t + 1) * P], w.qv[:, n, :],
                                    start=(n == 0), stop=(n == NC - 1))
                ins.then_inc(s_qv, 1)
            wait(pe, s_kb, b)
            for m in range(NC):
                for n in range(NC):
                    ins = pe.matmul(b_k[:, m * S:(m + 1) * S], w.k[:, n, m * P:(m + 1) * P], xnT[:, par, n, :],
                                    start=(n == 0), stop=(n == NC - 1))
            ins.then_inc(s_k, 1)

        def turn_kq(b, par):
            pe.wait_ge(s_ek, b + 1)
            wait(pe, s_onT, b - 1)
            for t in range(NT):
                for m in range(NC):
                    ins = pe.transpose(b_turn[1][:, t * D + m * P:t * D + (m + 1) * P],
                                       ek[:, par, m, t * P:(t + 1) * P], ident[:, :])
            ins.then_inc(s_ekP, 1)
            pe.wait_ge(s_eq, b + 1)
            pe.wait_ge(s_xnT, at_most(b + 2, NB))
            turn_over(pe, ident, eq[:, par], b_turn[0], s_eqP)

        def states(b, par):
            pe.wait_ge(s_ekN, b + 1)
            pe.wait_ge(s_qv_sb, (b + 1) * NT)
            wait(pe, s_state, b)
            for m in range(NC):
                for t in range(NT):
                    ins = pe.matmul(b_state[:, m * P:(m + 1) * P], ekN[:, t, m * P:(m + 1) * P],
                                    qv[:, par, t, D + m * P:D + (m + 1) * P], start=(t == 0), stop=(t == NT - 1))
            ins.then_inc(s_st, 1)

        def attend(b, par):
            pe.wait_ge(s_state, b + 1)
            pe.wait_ge(s_eqT, b + 1)
            wait(pe, s_osb, b)
            for t in range(NT):
                for m in range(NC):
                    ins = pe.matmul(b_out[:, t * D + m * P:t * D + (m + 1) * P], eqT[:, m, t * P:(t + 1) * P],
                                    state[:, m, :], start=True, stop=True)
            ins.then_inc(s_out, 1)

        def turn_o(b, par):
            pe.wait_ge(s_on, b + 1)
            pe.wait_ge(s_ekN, at_most(b + 2, NB))
            turn_over(pe, ident, on, b_turn[1], s_onP)

        def output(b, par):
            pe.wait_ge(s_onT, b + 1)
            wait(pe, s_add, b)
            for t in range(NT):
                for n in range(NC):
                    ins = pe.matmul(b_y[:, t * D:(t + 1) * D], onT[:, n, t * P:(t + 1) * P], w.o[:, n, :],
                                    start=(n == 0), stop=(n == NC - 1))
            ins.then_inc(s_y, 1)

        over_batches(pe, [(0, turn_x), (1, turn_kq), (0, project), (1, states), (2, turn_o), (1, attend),
                          (2, output)], depth=4)

    def scalar(act):

        def copy_x(b, par):
            act.wait_ge(s_xT, b + 1)
            wait(act, s_k, b - 1)
            act.activation(xnT[:, par].rearrange("p a b -> p (a b)"), b_turn[0][:, :], ACT.Copy).then_inc(s_xnT, 1)

        def copy_kq(b, par):
            act.wait_ge(s_ekP, b + 1)
            wait(act, s_st, b)
            act.activation(ekN[:, :, :].rearrange("p a b -> p (a b)"), b_turn[1][:, :], ACT.Copy).then_inc(s_ekN, 1)
            act.wait_ge(s_eqP, b + 1)
            wait(act, s_out, b)
            act.activation(eqT[:, :, :].rearrange("p a b -> p (a b)"), b_turn[0][:, :], ACT.Copy).then_inc(s_eqT, 1)

        def bias_k(b, par):
            wait_once(act, b, *w.loaded["la"])
            act.wait_ge(s_k, b + 1)
            wait(act, s_ek, b)
            for m in range(NC):
                ins = act.activation(kb[:, m, :], b_k[:, m * S:(m + 1) * S], ACT.Identity, bias=w.bk[:, m:m + 1])
            ins.then_inc(s_kb, 1)

        def exps(b, par):
            act.wait_ge(s_nmax, b + 1)
            wait(act, s_ekP, b - 1)
            wait(act, s_state, b - 1)
            for m in range(NC):
                ins = act.activation(ek[:, par, m, :], kb[:, m, :], ACT.Exp, bias=nmax[:, m:m + 1],
                                     accum_out=ksum[:, par, m:m + 1])
            ins.then_inc(s_ek, 1)
            act.wait_ge(s_qs, b + 1)
            wait(act, s_eqP, b - 1)
            wait(act, s_qsum, b - 1)
            act.activation(eq[:, par].rearrange("p a b -> p (a b)"), qs[:, :, :].rearrange("p a b -> p (a b)"),
                           ACT.Exp).then_inc(s_eq, 1)

        def copy_o(b, par):
            act.wait_ge(s_onP, b + 1)
            wait(act, s_y, b)
            for m in range(NC):
                ins = act.activation(onT[:, m, :], b_turn[1][:, m * S:(m + 1) * S], ACT.Identity,
                                     bias=w.ln_b[:, m:m + 1], scale=w.ln_g[:, m:m + 1])
            ins.then_inc(s_onT, 1)

        over_batches(act, [(0, copy_x), (1, copy_kq), (0, bias_k), (2, copy_o), (0, exps)], depth=4)

    def vector(dve):
        dve.wait_ge(w.s_const, 1)
        norm_x = ln.vector(dve, x, s_xT)
        q_ch, o_ch = Chain(dve, s_qch, NT), Chain(dve, s_och, 2 * NT)

        def norm(b, par):
            wait_x(dve, w, b)
            norm_x(b, par)

        def take_qv(b, par):
            wait_once(dve, b, *w.loaded["la"])
            for t in range(NT):
                dve.wait_ge(s_qv, b * NT + t + 1)
                if t == 0:
                    wait(dve, s_st, b - 1)
                dve.tensor_tensor(qv[:, par, t, :], b_qv[t][:, :], w.bqv[:, :], ALU.add).then_inc(s_qv_sb, 1)

        def softmax_start(b, par):
            dve.wait_ge(s_kb, b + 1)
            wait(dve, s_ek, b)
            dve.tensor_reduce(nmax[:, :], kb[:, :, :], AX.X, ALU.max, negate=True).then_inc(s_nmax, 1)
            q_ch.start(b)
            dve.wait_ge(s_qv_sb, (b + 1) * NT)
            for t in range(NT):
                last = q_ch.mark(dve.tensor_reduce(qmax[:, t * H:(t + 1) * H], heads(qv[:, par, t, 0:D]),
                                                   AX.X, ALU.max))
            dve.wait_ge(s_qch, last)
            wait(dve, s_eq, b)
            for t in range(NT):
                ins = dve.tensor_tensor(heads(qs[:, t, :]), heads(qv[:, par, t, 0:D]),
                                        spread(qmax[:, t * H:(t + 1) * H]), ALU.subtract)
            ins.then_inc(s_qs, 1)
            q_ch.end()

        def heads(v):
            return v.rearrange("p (h d) -> p h d", d=HD)

        def spread(v):
            return v.unsqueeze(2).broadcast_to([P, H, HD])

        def sum_q(b, par):
            dve.wait_ge(s_eq, b + 1)
            dve.tensor_reduce(qsum[:, :], eq[:, par].rearrange("p t (h d) -> p (t h) d", d=HD), AX.X,
                              ALU.add).then_inc(s_qsum, 1)
            dve.wait_ge(s_qsum, b + 1)
            dve.reciprocal(rq[:, :], qsum[:, :]).then_inc(s_rq, 1)
            dve.reciprocal(rks[:, :], ksum[:, par, :]).then_inc(s_rks, 1)

        def take_state(b, par):
            dve.wait_ge(s_st, b + 1)
            dve.wait_ge(s_rks, b + 1)
            wait(dve, s_out, b)
            for m in range(NC):
                ins = dve.scalar_tensor_tensor(out=state[:, m, :], in0=b_state[:, m * P:(m + 1) * P],
                                               scalar=rks[:, m:m + 1], in1=c.same_head[:, :], op0=ALU.mult, op1=ALU.mult)
            ins.then_inc(s_state, 1)

        def take_out(b, par):
            o_ch.start(b)
            dve.wait_ge(s_out, b + 1)
            dve.wait_ge(s_rq, b + 1)
            for t in range(NT):
                ins = dve.tensor_tensor(heads(o[:, t, :]), heads(b_out[:, t * D:(t + 1) * D]),
                                        spread(rq[:, t * H:(t + 1) * H]), ALU.mult)
            ins.then_inc(s_osb, 1)
            dve.wait_ge(s_osb, b + 1)
            for t in range(NT):
                last = o_ch.mark(dve.bn_stats(o_stats[:, t, :], o[:, t, :]))
            dve.wait_ge(s_och, last)
            c.alone(dve)
            for t in range(NT):
                last = o_ch.mark(dve.bn_aggr(o_mv[:, t, :], o_stats[:, t, :]))
            dve.wait_ge(s_och, last)
            dve.tensor_scalar(o_var[:, :], o_mv[:, :, 1], LN_EPS, None, ALU.add).then_inc(s_ovar, 1)
            dve.wait_ge(s_orstd, b + 1)
            wait(dve, s_onP, b)
            for t in range(NT):
                ins = dve.tensor_scalar(on[:, t, :], o[:, t, :], o_mv[:, t, 0:1], o_rstd[:, t:t + 1],
                                        ALU.subtract, ALU.mult)
            ins.then_inc(s_on, 1)
            o_ch.end()

        def add_y(b, par):
            dve.wait_ge(s_y, b + 1)
            dve.wait_ge(s_bo, b + 1)
            xb = batch_of(x, b)
            dve.tensor_tensor(xb, b_y[:, :].rearrange("p (t d) -> p t d", t=NT), xb, ALU.add).then_inc(s_add, 1)

        over_batches(dve, [(2, sum_q), (0, norm), (1, take_qv), (2, take_state), (1, softmax_start), (2, take_out),
                           (3, add_y)], depth=4, before_last=norm_ahead(c, dve, x, (s_xT, NB)))

    def gpsimd(pool):
        pool.wait_ge(w.s_const, 1)
        norm = ln.gpsimd(pool)

        def add_bo(b, par):
            wait_once(pool, b, *w.loaded["la"])
            pool.wait_ge(ln.s_xn, b + 1)
            for t in range(NT):
                xt = tile_of(x, b, t)
                ins = pool.tensor_tensor(xt, xt, w.bo[:, :].unsqueeze(1), ALU.add)
            ins.then_inc(s_bo, 1)

        def constants(b, par):
            if isinstance(b, int) and b == 0:
                c.later_constants(pool)

        def norm_o(b, par):
            pool.wait_ge(s_ovar, b + 1)
            pool.tensor_tensor(o_rstd[:, :], o_var[:, :], c.minus_half[:, 0:NT], ALU.pow).then_inc(s_orstd, 1)

        over_batches(pool, [(0, norm), (1, add_bo), (1, constants), (2, norm_o)], depth=4)
        norm_ahead(c, pool, x)()

    return {"norm": ln, "tensor": tensor, "scalar": scalar, "vector": vector, "gpsimd": gpsimd}


def cross_attention(c, x, w):
    H, HD = 16, 16
    SCALE = 1.0 / HD ** 0.5
    Q_PART, K_PART = (0, 0, 0, 1, 1, 2), (0, 1, 2, 0, 1, 0)
    ROWS = len(Q_PART) * HD
    VW = 32
    QUADS = (0, 2, 1, 3)
    ORDER = [4 * a + j for a in QUADS for j in range(4)]
    N_DMA = len(Q_PART) + len(K_PART)
    PT_RING = 8

    def place(h):
        return (h % 8) * 2 + h // 8

    banks, ident, ident_bf = c.banks, c.ident, c.ident_bf
    c.new_stage()
    ln = LayerNorm(c, "ca")
    xnT = c.take([P, NC, S])
    ctxv = c.take([P, 2, NC, S])
    qp, kp = c.take([P, 2, 3, NC * S], BF16), c.take([P, 2, 3, NC * S], BF16)
    qr, kr = c.take([P, NC * S]), c.take([P, NC * S])
    q6, k6 = c.take([P, 2, H, S], BF16), c.take([P, 2, H, S], BF16)
    v32 = c.take([P, 2, NT, H, VW])
    mx = c.take([P, NT, H])
    em = c.take([P, 2, NT, H])
    m_res = c.take([P, NT, H])
    m_parts = c.take([P, NT, 3 * H], BF16)
    m_rows = c.take([P, S], BF16)
    junk = c.take([P, 2, 3 * P])
    pt = c.take([P, PT_RING, 3 * P])
    oT = c.take([P, 4, S])
    later = c.take([P, 2, NT, D])
    den, rden = c.take([P, NT, H]), c.take([P, NT, H])
    y = c.take([P, NT, D])

    b_s, b_st = [banks[0], banks[1]], [banks[2], banks[3], banks[4]]
    bank_a, bank_b, bank_c = banks[5], banks[6], banks[7]

    sem = lambda n: c.sem("ca_" + n)
    s_init = sem("init")
    s_ctxv = [sem("ctxv0"), sem("ctxv1")]
    s_xT, s_xnT = sem("xT"), sem("xnT")
    s_q, s_k, s_v = sem("q"), sem("k"), sem("v")
    s_q1, s_k1 = sem("q1"), sem("k1")
    s_qr, s_kr = sem("qr"), sem("kr")
    s_q2, s_k2 = sem("q2"), sem("k2")
    s_qp, s_kp = sem("qp"), sem("kp")
    s_half = [sem("half0"), sem("half1")]
    s_sc = sem("scores")
    s_mx = sem("mx")
    s_mch = sem("m_chain")
    s_mp = sem("m_parts")
    s_mT = sem("mT")
    s_mrow = sem("m_rows")
    s_mland = c.lasting_sem("ca_m_landed")
    s_em = sem("em")
    s_v32 = sem("v32")
    s_st = sem("st")
    s_exp = sem("exp")
    s_pv = sem("pv")
    s_ot = [sem("ot0"), sem("ot1")]
    s_suf, s_later = sem("suf"), sem("later")
    s_on = [sem("on0"), sem("on1")]
    s_den = sem("den")
    s_sum = [sem("sum0"), sem("sum1")]
    s_rden = sem("rden")
    s_y = sem("y")
    s_add = sem("add")

    def sync(sp):
        def load_ctx(b, par):
            wait(sp, s_v, b - 1)
            src = c.ins["ctx_T"]
            src = src[b] if isinstance(b, int) else src[bass.ds(b, 1)].rearrange("o d s -> (o d) s")
            sp.dma_start(ctxv[:, par], src.rearrange("(n p) s -> p n s", p=P)).then_inc(s_ctxv[par], 16)

        def stack(b, par):
            sp.wait_ge(s_qp, b + 1)
            sp.wait_ge(s_kp, b + 1)
            for half in range(2):
                wait(sp, s_st, b * H - 2 * H + (half + 1) * H // 2)
                c.alone(sp)
                wait(sp, s_half[half], 16 * N_DMA * b)
                rows_of = slice(half * P // 2, (half + 1) * P // 2)
                for dst, src, part in ((q6, qp, Q_PART), (k6, kp, K_PART)):
                    for r, k in enumerate(part):
                        sp.dma_start(dst[r * HD:(r + 1) * HD, par, half * H // 2:(half + 1) * H // 2, :],
                                     src[rows_of, par, k, :]).then_inc(s_half[half], 16)

        over_batches(sp, [(1, load_ctx), (0, stack)], depth=4)

    def tensor(pe):
        wait_weights(pe, w, "ca")

        def turn_m(b, par):
            pe.wait_ge(s_mp, b + 1)
            wait(pe, s_later, b)
            pe.wait_ge(s_kr, at_most(b + 2, NB))
            c.alone(pe)
            for t in range(NT):
                ins = pe.transpose(bank_a[0:3 * H, 0:P].bitcast(BF16)[:, t * P:(t + 1) * P],
                                   m_parts[:, t, :], ident_bf[:, :])
            ins.then_inc(s_mT, 1)

        def project_v(b, par):
            pe.wait_ge(s_ctxv[par], 16 + 8 * (b - par))
            wait(pe, s_ot[1], b)
            pe.wait_ge(s_xnT, at_most(b + 2, NB))
            for t in range(NT):
                for n in range(NC):
                    ins = pe.matmul(bank_b[:, t * D:(t + 1) * D], ctxv[:, par, n, t * P:(t + 1) * P], w.cv[:, n, :],
                                    start=(n == 0), stop=(n == NC - 1))
            ins.then_inc(s_v, 1)

        def project_k(b, par):
            wait(pe, s_mrow, b - 1)
            wait(pe, s_kr, b)
            src = c.ctxT[:, :, bass.ds(b * S, S)] if not isinstance(b, int) else c.ctxT[:, :, b * S:(b + 1) * S]
            for m in range(NC):
                for n in range(NC):
                    ins = pe.matmul(bank_a[:, m * S:(m + 1) * S], w.ck[:, n, m * P:(m + 1) * P], src[:, n, :],
                                    start=(n == 0), stop=(n == NC - 1))
            ins.then_inc(s_k, 1)

        def turn_x(b, par):
            pe.wait_ge(ln.s_xn, b + 1)
            wait(pe, s_v32, b - 1)
            wait(pe, s_xnT, b)
            turn_over(pe, ident, ln.xn[:, par], bank_b, s_xT)

        def suffix(b, par):
            pe.wait_ge(s_v32, b + 1)
            pe.wait_ge(s_mrow, b + 1)
            pe.wait_ge(s_kr, at_most(b + 3, NB))
            for t in range(NT):
                for k in range(t, NT):
                    ins = pe.matmul(bank_a[:, t * D:(t + 1) * D], c.after[:, :] if k == t else c.ones[:, :],
                                    v32[:, par, k, :, 0:HD], start=(k == t), stop=(k == NT - 1))
            ins.then_inc(s_suf, 1)

        def project_q(b, par):
            pe.wait_ge(s_xnT, b + 1)
            wait(pe, s_ot[0], b - 2)
            wait(pe, s_qr, b)
            for m in range(NC):
                for n in range(NC):
                    ins = pe.matmul(bank_c[:, m * S:(m + 1) * S], w.cq[:, n, m * P:(m + 1) * P], xnT[:, n, :],
                                    start=(n == 0), stop=(n == NC - 1))
            ins.then_inc(s_q, 1)

        def turn_o(b, par):
            for half in range(2):
                pe.wait_ge(s_ot[half], b + 1)
            pe.wait_ge(s_qr, at_most(b + 4, NB))
            pe.wait_ge(s_xnT, at_most(b + 4, NB))
            pe.wait_ge(s_v32, at_most(b + 2, NB))
            for t, bank in enumerate((bank_c, bank_b)):
                for a in range(4):
                    ins = pe.transpose(bank[:, a * P:(a + 1) * P], oT[:, a, t * P:(t + 1) * P], ident[:, :])
                ins.then_inc(s_on[t], 1)

        def scores(b, par, n):
            g = place(ORDER[n])
            if n % (H // 2) == 0:
                half = n // (H // 2)
                pe.wait_ge(s_half[half], 16 * N_DMA * (b + 1))
            wait(pe, s_mx, b * H + n - 1)
            bank = b_s[n % 2]
            pe.matmul(bank[:, 0:P], q6[0:ROWS, par, g, 0:P], k6[0:ROWS, par, g, 0:P], start=True, stop=True)
            pe.matmul(bank[:, P:3 * P], q6[0:ROWS, par, g, P:S], k6[0:ROWS, par, g, :],
                      start=True, stop=True).then_inc(s_sc, 1)

        def scores_T(b, par, n):
            g = place(ORDER[n])
            if n == 0:
                wait_once(pe, b, s_init, 3)
                pe.wait_ge(s_mland, 48 * (b + 1))
            wait(pe, s_exp, b * H + (n - 2 if n >= 3 else (0, -2, -1)[n]))
            bank = b_st[n % 3]
            top = ROWS + 3
            pe.matmul(bank[:, 0:S], k6[0:top, par, g, 0:P], q6[0:top, par, g, :], start=True, stop=False,
                      skip_group_check=True)
            pe.matmul(bank[:, S:3 * P], k6[0:top, par, g, P:S], q6[0:top, par, g, P:S], start=False, stop=False,
                      skip_group_check=True)
            diagonal = bank[:, :].rearrange("p (a b) -> p a b", b=P)[:, 0:3:2, :]
            pe.matmul(diagonal, ident_bf[:, :], c.masked[:, :, :], start=False, stop=True,
                      skip_group_check=True).then_inc(s_st, 1)

        def values(b, par, i):
            if i == 0:
                pe.wait_ge(s_v32, b + 1)
                wait(pe, s_sum[0], b)
                pe.wait_ge(s_qr, at_most(b + 3, NB))
            if i == 2:
                wait(pe, s_sum[1], b)
                pe.wait_ge(s_xnT, at_most(b + 3, NB))
            pe.wait_ge(s_exp, b * H + 4 * i + 4)
            bank, col = (bank_c, bank_b)[i // 2], (i % 2) * S
            for k in range(NT):
                for j in range(4):
                    h = 4 * QUADS[i] + j
                    p = pt[:, (4 * i + j) % PT_RING, :]
                    ins = pe.matmul(bank[VW * j:VW * (j + 1), col + k * P:col + S], v32[:, par, k, h, :],
                                    p[:, 0:S] if k == 0 else p[:, S:3 * P], start=(k == 0), stop=(k == NT - 1),
                                    skip_group_check=True)
            ins.then_inc(s_pv, 1)

        def heads(b_max, b_exp, par):
            for n in range(H):
                if b_max is not None:
                    scores(b_max, 1 - par, n)
                if b_exp is not None:
                    scores_T(b_exp, par, n)
                    if n % 4 == 1 and n > 4:
                        values(b_exp, par, n // 4 - 1)
            if b_exp is not None:
                values(b_exp, par, 3)

        def both(b, par):
            last = isinstance(b, int) and b == NB - 1
            heads(None if last else b + 1, b, par)

        def first(b, par):
            if isinstance(b, int) and b == 0:
                heads(b, None, 1 - par)

        over_batches(pe, [(2, turn_m), (2, project_v), (0, project_k), (0, turn_x), (0, project_q), (2, suffix),
                          (3, turn_o), (1, first), (2, both)], depth=4)

    def scalar(act):
        wait_weights(act, w, "ca")
        act.wait_ge(w.s_const, 2)

        def ones_under_k(par):
            rows = k6[ROWS:P, par].rearrange("p h s -> p (h s)")
            act.activation(rows, c.ones[ROWS:P, 0:1].broadcast_to([P - ROWS, H * S]), ACT.Copy).then_inc(s_init, 1)

        ones_under_k(0)

        def copy_m(b, par):
            act.wait_ge(s_mT, b + 1)
            wait(act, s_mland, 48 * b)
            act.activation(m_rows[0:3 * H, :], bank_a[0:3 * H, 0:P].bitcast(BF16), ACT.Copy).then_inc(s_mrow, 1)
            wait(act, s_sum[1], b - 1)
            act.activation(em[:, par], mx[:, :, :], ACT.Exp, scale=-SCALE).then_inc(s_em, 1)

        def copy_v(b, par):
            act.wait_ge(s_v, b + 1)
            wait_once(act, b, s_init, 3)
            wait(act, s_pv, 4 * (b - 1))
            wait(act, s_suf, b - 1)
            act.activation(v32[:, par, :, :, 0:HD], bank_b[:, :].rearrange("p (t h d) -> p t h d", t=NT, h=H),
                           ACT.Copy).then_inc(s_v32, 1)

        def part_1(bank, parts, s_in, s_out, b, par):
            act.wait_ge(s_in, b + 1)
            for half in range(2):
                wait(act, s_half[half], 16 * N_DMA * (b - 1))
            act.activation(parts[:, par, 0, :], bank[:, :], ACT.Copy).then_inc(s_out, 1)

        def part_2(res, parts, s_in, s_out, b, par):
            act.wait_ge(s_in, b + 1)
            act.activation(parts[:, par, 1, :], res[:, :], ACT.Copy).then_inc(s_out, 1)

        def split_k(b, par):
            part_1(bank_a, kp, s_k, s_k1, b, par)

        def copy_x(b, par):
            act.wait_ge(s_xT, b + 1)
            wait(act, s_q, b)
            act.activation(xnT[:, :, :].rearrange("p a b -> p (a b)"), bank_b[:, :], ACT.Copy).then_inc(s_xnT, 1)
            part_2(kr, kp, s_kr, s_k2, b, par)

        def split_q(b, par):
            part_1(bank_c, qp, s_q, s_q1, b, par)
            part_2(qr, qp, s_qr, s_q2, b, par)
            if isinstance(b, int) and b == 0:
                ones_under_k(1)

        def exps(b, par):
            for n in range(H):
                act.wait_ge(s_st, b * H + n + 1)
                wait(act, s_pv, b * 4 + n // 4 - 1)
                act.activation(pt[:, n % PT_RING, :], b_st[n % 3][:, 0:3 * P], ACT.Exp, scale=SCALE).then_inc(s_exp, 1)
                if n == 11:
                    copy_o(b, 0)
            copy_o(b, 1)

        def copy_o(b, half):
            act.wait_ge(s_pv, b * 4 + 2 * half + 2)
            wait(act, s_on[1], b)
            bank = (bank_c, bank_b)[half]
            act.activation(oT[:, half:half + 3:2, :], bank[:, :].rearrange("p (a s) -> p a s", a=2),
                           ACT.Copy).then_inc(s_ot[half], 1)

        over_batches(act, [(2, copy_m), (2, copy_v), (0, split_k), (0, copy_x), (0, split_q), (2, exps)], depth=4)

    def vector(dve):
        wait_weights(dve, w, "ca")
        norm_x = ln.vector(dve, x, s_xT)
        m_ch = Chain(dve, s_mch, 3)

        def norm(b, par):
            wait_x(dve, w, b)
            norm_x(b, par)

        def rest(bank, parts, res, s_in, s_free, s_out, b, par):
            dve.wait_ge(s_in, b + 1)
            wait(dve, s_free, b)
            dve.tensor_tensor(res[:, :], bank[:, :], parts[:, par, 0, :], ALU.subtract).then_inc(s_out, 1)

        def rest_k(b, par):
            rest(bank_a, kp, kr, s_k1, s_kp, s_kr, b, par)

        def rest_q(b, par):
            rest(bank_c, qp, qr, s_q1, s_qp, s_qr, b, par)

        def take_suffix(b, par):
            dve.wait_ge(s_suf, b + 1)
            dve.wait_ge(s_em, b + 1)
            wait(dve, s_y, b - 1)
            for t in range(NT):
                ins = dve.tensor_tensor(later[:, par, t, :].rearrange("p (h d) -> p h d", d=HD),
                                        bank_a[:, t * D:(t + 1) * D].rearrange("p (h d) -> p h d", d=HD),
                                        em[:, par, t, :].unsqueeze(2).broadcast_to([P, H, HD]), ALU.mult)
            ins.then_inc(s_later, 1)

        def take_on(b, par):
            dve.wait_ge(s_later, b + 1)
            wait(dve, s_y, b)
            for t, bank in enumerate((bank_c, bank_b)):
                dve.wait_ge(s_on[t], b + 1)
                on = bank[:, :].rearrange("p (h v) -> p h v", v=VW)
                dve.scalar_tensor_tensor(out=den[:, t, :], in0=em[:, par, t, :], scalar=c.n_after[:, t:t + 1],
                                         in1=on[:, :, HD], op0=ALU.mult, op1=ALU.add).then_inc(s_den, 1)
                acc = later[:, par, t, :].rearrange("p (h d) -> p h d", d=HD)
                dve.tensor_tensor(acc, acc, on[:, :, 0:HD], ALU.add).then_inc(s_sum[t], 1)
            dve.wait_ge(s_den, NT * (b + 1))
            dve.reciprocal(rden[:, :, :], den[:, :, :]).then_inc(s_rden, 1)

        def maxima(b, par):
            wait(dve, s_em, b)
            for n in range(H):
                dve.wait_ge(s_sc, b * H + n + 1)
                wait(dve, s_mx, b * H + n - 1)
                c.alone(dve)
                h, bank = ORDER[n], b_s[n % 2]
                dve.tensor_tensor_reduce(out=junk[:, n % 2, 0:P], in0=bank[:, 0:P], in1=c.causal[:, 0:P], scale=1.0,
                                         scalar=0.0, op0=ALU.mult, op1=ALU.max, accum_out=mx[:, 0, h:h + 1])
                dve.tensor_tensor_reduce(out=junk[:, n % 2, P:3 * P], in0=bank[:, P:3 * P], in1=c.causal[:, P:3 * P], scale=1.0,
                                         scalar=NEG, op0=ALU.mult, op1=ALU.max,
                                         accum_out=mx[:, 1, h:h + 1]).then_inc(s_mx, 1)
            by_place = lambda v: v.rearrange("p t (j h) -> p t h j", h=8)
            part = lambda k: m_parts[:, :, k * H:(k + 1) * H].rearrange("p t (h j) -> p t h j", j=2)
            res = m_res[:, :, :].rearrange("p t (h j) -> p t h j", j=2)
            m_ch.start(b)
            wait(dve, s_mT, b)
            dve.wait_ge(s_mx, (b + 1) * H)
            for t in range(NT):
                last = dve.tensor_scalar(part(0)[:, t], by_place(mx)[:, t], -1.0, None, ALU.mult)
            m_ch.link(last)
            for t in range(NT):
                last = dve.scalar_tensor_tensor(out=res[:, t], in0=by_place(mx)[:, t], scalar=-1.0,
                                                in1=part(0)[:, t], op0=ALU.mult, op1=ALU.subtract)
            m_ch.link(last)
            for t in range(NT):
                last = dve.tensor_copy(part(1)[:, t], res[:, t])
            m_ch.link(last)
            for t in range(NT):
                last = dve.tensor_tensor(part(2)[:, t], res[:, t], part(1)[:, t], ALU.subtract)
            last.then_inc(s_mp, 1)
            m_ch.end()

        over_batches(dve, [(0, norm), (1, rest_k), (1, rest_q), (3, take_suffix), (4, take_on), (2, maxima)], depth=6,
                     before_last=norm_ahead(c, dve, x, (s_xT, NB), (s_add, AHEAD)))

    def gpsimd(pool):
        wait_weights(pool, w, "ca")
        norm = ln.gpsimd(pool)
        pool.memset(v32[:, :, :, :, HD:VW], 0.0).then_inc(s_init0, 1)
        pool.wait_ge(s_init0, 1)
        pool.memset(v32[:, :, :, :, HD:HD + 1], 1.0).then_inc(s_init, 1)

        def part_3(res, parts, s_in, s_out, b, par):
            pool.wait_ge(s_in, b + 1)
            for half in range(2):
                wait(pool, s_half[half], 16 * N_DMA * (b - 1))
            pool.tensor_tensor(parts[:, par, 2, :], res[:, :], parts[:, par, 1, :], ALU.subtract).then_inc(s_out, 1)

        def part_k(b, par):
            part_3(kr, kp, s_k2, s_kp, b, par)

        def part_q(b, par):
            part_3(qr, qp, s_q2, s_qp, b, par)

        def send_m(b, par):
            pool.wait_ge(s_mrow, b + 1)
            c.alone(pool)
            for k in range(3):
                pool.dma_start(q6[ROWS + k:ROWS + k + 1, par], m_rows[k * H:(k + 1) * H, :]).then_inc(s_mland, 16)

        def add_y(b, par):
            pool.wait_ge(s_rden, b + 1)
            wait(pool, s_add, b)
            for t in range(NT):
                pool.wait_ge(s_sum[t], b + 1)
                ins = pool.tensor_tensor(y[:, t, :].rearrange("p (h d) -> p h d", d=HD),
                                         later[:, par, t, :].rearrange("p (h d) -> p h d", d=HD),
                                         rden[:, t, :].unsqueeze(2).broadcast_to([P, H, HD]), ALU.mult)
            ins.then_inc(s_y, 1)
            pool.wait_ge(s_y, b + 1)
            xb = batch_of(x, b)
            pool.tensor_tensor(xb, xb, y[:, :, :], ALU.add).then_inc(s_add, 1)

        over_batches(pool, [(0, norm), (3, send_m), (1, part_k), (1, part_q), (4, add_y)], depth=6, before_last=norm_ahead(c, pool, x))

    s_init0 = sem("init0")
    return {"norm": ln, "sync": sync, "tensor": tensor, "scalar": scalar, "vector": vector, "gpsimd": gpsimd}


def low_rank_ffn(c, x, w):
    R, F = 64, 1024
    NF = F // P
    banks, ident = c.banks, c.ident
    c.new_stage()
    ln = LayerNorm(c, "lf")
    xnT = c.take([P, NC, S])
    pT = c.take([P, S])
    hT = c.take([P, NF, S])
    qT = c.take([P, S])

    b_x, b_p, b_q, b_y = banks[0], banks[1], banks[6], banks[7]
    b_h = banks[2:6]

    sem = lambda n: c.sem("lf_" + n)
    s_xT, s_xnT, s_p, s_pT = sem("xT"), sem("xnT"), sem("p"), sem("pT")
    s_h, s_gelu = sem("h"), sem("gelu")
    s_q, s_qT, s_y, s_add, s_b2 = sem("q"), sem("qT"), sem("y"), sem("add"), sem("b2")

    def tensor(pe):
        wait_weights(pe, w, "lf")

        def turn_x(b, par):
            pe.wait_ge(ln.s_xn, b + 1)
            wait(pe, s_xnT, b)
            turn_over(pe, ident, ln.xn[:, par], b_x, s_xT)

        def into_rank(b, par):
            pe.wait_ge(s_xnT, b + 1)
            wait(pe, s_pT, b)
            for n in range(NC):
                ins = pe.matmul(b_p[:, 0:S], w.u1[:, n, :], xnT[:, n, :], start=(n == 0), stop=(n == NC - 1))
            ins.then_inc(s_p, 1)

        def hidden(b, par):
            pe.wait_ge(s_pT, b + 1)
            for f in range(NF):
                if f % 2 == 0:
                    wait(pe, s_gelu, (b - 1) * NF + f + 2)
                ins = pe.matmul(b_h[f // 2][:, f % 2 * S:(f % 2 + 1) * S], w.v1[:, f * P:(f + 1) * P], pT[:, :],
                                start=True, stop=True)
                if f % 2 == 1:
                    ins.then_inc(s_h, 1)

        def out_of_hidden(b, par):
            pe.wait_ge(s_gelu, (b + 1) * NF)
            wait(pe, s_qT, b)
            for f in range(0, NF, 2):
                for odd in range(2):
                    ins = pe.matmul(b_q[odd * R:(odd + 1) * R, 0:S], w.u2[:, f + odd, :], hT[:, f + odd, :],
                                    start=(f == 0), stop=(f == NF - 2), skip_group_check=True)
            ins.then_inc(s_q, 1)

        def output(b, par):
            pe.wait_ge(s_qT, b + 1)
            wait(pe, s_add, b)
            for t in range(NT):
                ins = pe.matmul(b_y[:, t * D:(t + 1) * D], qT[:, t * P:(t + 1) * P], w.v2[:, :], start=True, stop=True)
            ins.then_inc(s_y, 1)

        over_batches(pe, [(0, turn_x), (1, out_of_hidden), (0, into_rank), (1, output), (0, hidden)])

    def scalar(act):
        wait_weights(act, w, "lf")

        def copy_x(b, par):
            act.wait_ge(s_xT, b + 1)
            wait(act, s_p, b)
            act.activation(xnT[:, :, :].rearrange("p a b -> p (a b)"), b_x[:, :], ACT.Copy).then_inc(s_xnT, 1)

        def copy_p(b, par):
            act.wait_ge(s_p, b + 1)
            wait(act, s_h, b * NF // 2)
            act.activation(pT[:, :], b_p[:, 0:S], ACT.Copy).then_inc(s_pT, 1)

        def copy_q(b, par):
            act.wait_ge(s_q, b + 1)
            wait(act, s_y, b)
            act.activation(qT[:, :], b_q[:, 0:S], ACT.Copy).then_inc(s_qT, 1)

        def gelus(b, par):
            wait(act, s_q, b)
            for f in range(NF):
                if f % 2 == 0:
                    act.wait_ge(s_h, b * (NF // 2) + f // 2 + 1)
                act.activation(hT[:, f, :], b_h[f // 2][:, f % 2 * S:(f % 2 + 1) * S], ACT.Gelu_apprx_tanh,
                               bias=w.fb1[:, f:f + 1]).then_inc(s_gelu, 1)

        over_batches(act, [(0, copy_x), (1, copy_q), (0, copy_p), (0, gelus)])

    def vector(dve):
        norm_x = ln.vector(dve, x, s_xT)

        def norm(b, par):
            wait_x(dve, w, b)
            norm_x(b, par)

        def add_y(b, par):
            dve.wait_ge(s_y, b + 1)
            dve.wait_ge(s_b2, b + 1)
            xb = batch_of(x, b)
            dve.tensor_tensor(xb, b_y[:, :].rearrange("p (t d) -> p t d", t=NT), xb, ALU.add).then_inc(s_add, 1)

        over_batches(dve, [(0, norm), (2, add_y)], before_last=norm_ahead(c, dve, x, (s_xT, NB)))

    def gpsimd(pool):
        wait_weights(pool, w, "lf")
        norm = ln.gpsimd(pool)

        def add_b2(b, par):
            pool.wait_ge(ln.s_xn, b + 1)
            for t in range(NT):
                xt = tile_of(x, b, t)
                ins = pool.tensor_tensor(xt, xt, w.fb2[:, :].unsqueeze(1), ALU.add)
            ins.then_inc(s_b2, 1)

        over_batches(pool, [(0, norm), (0, add_b2)], depth=2)
        norm_ahead(c, pool, x)()

    return {"norm": ln, "tensor": tensor, "scalar": scalar, "vector": vector, "gpsimd": gpsimd}


def causal_linear_attention(c, x, w):
    K = 64
    EPS = 1e-6
    banks, ident = c.banks, c.ident
    c.new_stage()
    ln = LayerNorm(c, "cl")
    xnT = c.take([P, 2, NC, S])
    low = c.take([K, 2, S])
    e = c.take([K, 2, S])
    qk = c.take([P, 2, 2, S])
    vp = c.take([P, 2, NT, P])
    at = c.take([P, 3 * P])
    nT = c.take([P, 2, S])
    den, rden = c.take([P, NT]), c.take([P, NT])

    b_x, b_qk, b_v, b_at, b_n = banks[0:5]
    b_y = banks[5:7]

    sem = lambda n: c.sem("cl_" + n)
    s_init = sem("init")
    s_xT, s_xnT, s_qk, s_v = sem("xT"), sem("xnT"), sem("qk"), sem("v")
    s_low, s_e, s_feat, s_vp = sem("low"), sem("e"), sem("features"), sem("vp")
    s_at, s_masked, s_n, s_nT = sem("at"), sem("masked"), sem("n"), sem("nT")
    s_y, s_den, s_rden, s_add = sem("y"), sem("den"), sem("rden"), sem("add")

    def tensor(pe):
        wait_weights(pe, w, "cl")

        def turn_x(b, par):
            pe.wait_ge(ln.s_xn, b + 1)
            wait(pe, s_xnT, b)
            turn_over(pe, ident, ln.xn[:, par], b_x, s_xT)

        def scores(b, par):
            wait_once(pe, b, s_init, 2)
            pe.wait_ge(s_feat, b + 1)
            wait(pe, s_masked, b)
            pe.matmul(b_at[:, 0:S], qk[:, par, 1, 0:P], qk[:, par, 0, :], start=True, stop=True)
            pe.matmul(b_at[:, S:3 * P], qk[:, par, 1, P:S], qk[:, par, 0, P:S], start=True, stop=True)\
                .then_inc(s_at, 1)

        def output(b, par):
            pe.wait_ge(s_nT, b + 1)
            wait(pe, s_add, b)
            for t in range(NT):
                ins = pe.matmul(b_y[t][:, 0:D + 2], nT[:, par, t * P:(t + 1) * P], w.lo[:, :], start=True, stop=True)
            ins.then_inc(s_y, 1)

        def project(b, par):
            pe.wait_ge(s_xnT, b + 1)
            wait(pe, s_feat, b)
            for m in range(2):
                for n in range(NC):
                    ins = pe.matmul(b_qk[:, m * S:(m + 1) * S], w.lqk[:, n, m, :], xnT[:, par, n, :],
                                    start=(n == 0), stop=(n == NC - 1))
            ins.then_inc(s_qk, 1)
            wait(pe, s_vp, b)
            for t in range(NT):
                for n in range(NC):
                    ins = pe.matmul(b_v[:, t * P:(t + 1) * P], xnT[:, par, n, t * P:(t + 1) * P], w.lv[:, n, :],
                                    start=(n == 0), stop=(n == NC - 1))
            ins.then_inc(s_v, 1)

        def numerators(b, par):
            pe.wait_ge(s_masked, b + 1)
            pe.wait_ge(s_vp, b + 1)
            wait(pe, s_nT, b)
            pe.matmul(b_n[:, 0:S], vp[:, par, 0, :], at[:, 0:S], start=True, stop=False, skip_group_check=True)
            pe.matmul(b_n[:, P:S], vp[:, par, 1, :], at[:, S:3 * P], start=False, stop=True,
                      skip_group_check=True).then_inc(s_n, 1)

        over_batches(pe, [(0, turn_x), (1, scores), (0, project), (2, output), (1, numerators)], depth=4)

    def scalar(act):

        def copy_x(b, par):
            act.wait_ge(s_xT, b + 1)
            wait(act, s_v, b - 1)
            act.activation(xnT[:, par].rearrange("p a b -> p (a b)"), b_x[:, :], ACT.Copy).then_inc(s_xnT, 1)

        def copy_n(b, par):
            act.wait_ge(s_n, b + 1)
            wait(act, s_y, b - 1)
            act.activation(nT[:, par, :], b_n[:, 0:S], ACT.Copy).then_inc(s_nT, 1)

        def features(b, par):
            act.wait_ge(s_low, b + 1)
            wait(act, s_feat, b)
            act.activation(e[:, :, :].rearrange("p a b -> p (a b)"), low[:, :, :].rearrange("p a b -> p (a b)"),
                           ACT.Exp).then_inc(s_e, 1)
            act.wait_ge(s_v, b + 1)
            wait_once(act, b, s_init, 2)
            wait(act, s_n, b - 1)
            act.activation(vp[:, par, :, 0:K], b_v[:, 0:NT * P].rearrange("p (t m) -> p t m", t=NT)[:, :, 0:K],
                           ACT.Copy).then_inc(s_vp, 1)

        over_batches(act, [(0, copy_x), (0, features), (1, copy_n)], depth=4)

    def vector(dve):
        norm_x = ln.vector(dve, x, s_xT)
        dve.memset(qk[K:P], 0.0).then_inc(s_init, 1)

        def norm(b, par):
            wait_x(dve, w, b)
            norm_x(b, par)

        def features(b, par):
            z = b_qk[0:K, :].rearrange("p (m s) -> p m s", m=2)
            dve.wait_ge(s_qk, b + 1)
            wait(dve, s_e, b)
            dve.tensor_scalar(low[:, :, :], z, 0.0, None, ALU.min).then_inc(s_low, 1)
            dve.wait_ge(s_e, b + 1)
            wait(dve, s_at, b - 1)
            dve.scalar_tensor_tensor(out=qk[0:K, par], in0=z, scalar=0.0, in1=e[:, :, :], op0=ALU.max,
                                     op1=ALU.add).then_inc(s_feat, 1)

        def mask(b, par):
            dve.wait_ge(s_at, b + 1)
            wait(dve, s_n, b)
            dve.tensor_tensor(at[:, :], b_at[:, 0:3 * P], c.causal_T[:, :], ALU.mult).then_inc(s_masked, 1)

        def add_y(b, par):
            dve.wait_ge(s_y, b + 1)
            for t in range(NT):
                ins = dve.tensor_scalar(den[:, t:t + 1], b_y[t][:, D:D + 1], EPS, None, ALU.add)
            ins.then_inc(s_den, 1)
            dve.wait_ge(s_den, b + 1)
            dve.reciprocal(rden[:, :], den[:, :]).then_inc(s_rden, 1)
            dve.wait_ge(s_rden, b + 1)
            for t in range(NT):
                xt = tile_of(x, b, t).squeeze(1)
                ins = dve.scalar_tensor_tensor(out=xt, in0=b_y[t][:, 0:D], scalar=rden[:, t:t + 1], in1=xt,
                                               op0=ALU.mult, op1=ALU.add)
            ins.then_inc(s_add, 1)

        over_batches(dve, [(0, norm), (2, mask), (1, features), (3, add_y)], depth=4, before_last=norm_ahead(c, dve, x, (s_xT, NB)))

    def gpsimd(pool):
        norm = ln.gpsimd(pool)
        pool.memset(vp[:, :, :, K:P], 0.0).then_inc(s_init0, 1)
        pool.wait_ge(s_init0, 1)
        pool.memset(vp[:, :, :, K:K + 1], 1.0).then_inc(s_init, 1)
        over_batches(pool, [(0, norm)], depth=2)
        norm_ahead(c, pool, x)()

    s_init0 = sem("init0")
    return {"norm": ln, "tensor": tensor, "scalar": scalar, "vector": vector, "gpsimd": gpsimd}


def gated_attention(c, x, w):
    H, HD = 8, 32
    G = NB * H
    SCALE = 1.0 / HD ** 0.5
    EPS = 1e-6
    VW = 64
    WIN = G - H
    banks, ident, ident_bf = c.banks, c.ident, c.ident_bf
    c.new_stage()
    ln = LayerNorm(c, "ga")
    xnT = c.take([P, NC, NB * S])
    gb = c.take([P, S])
    neg, e, lsig = c.take([P, S]), c.take([P, S]), c.take([P, S])
    lf = c.take([P, S])
    iF = c.take([P, S])
    g, F = c.take([P, S]), c.take([P, S])
    M, zeros = c.take([P, S]), c.take([P, S])
    fm, en = c.take([P, S]), c.take([P, S])
    m_res = c.take([P, S])
    n1, n2, n3 = c.take([P, S], BF16), c.take([P, S], BF16), c.take([P, S], BF16)
    m12, m3 = c.take([P, 3 * P], BF16), c.take([P, 3 * P], BF16)
    gT, enT = c.take([P, NT, G]), c.take([P, NT, G])
    qz = c.take([P, 2, 4, NC, S])
    kT = c.take([P, 2, NC, S])
    v_in = c.take([P, 2, NT, D])
    v64 = c.take([P, 2, NT, H, VW])
    DT_RING, CT_RING = 4, 4
    dt = c.take([P, DT_RING, 3 * P])
    ct = c.take([P, CT_RING, 3 * P])
    oT = c.take([P, 4, S])
    total, mean, rn, r2, ssq, var, var2, rr = [c.take([P, NT, H]) for _ in range(8)]
    d = c.take([P, NT, D])
    sq = c.take([P, NT, D])
    y, z = c.take([P, NT, D]), c.take([P, NT, D])

    b_turn, b_gates, b_post = [banks[0], banks[1]], banks[2], banks[3]
    b_qk, b_d = [banks[4], banks[5]], [banks[6], banks[7]]
    b_o, b_on = [banks[0], banks[1]], [banks[2], banks[3]]

    sem = lambda n: c.sem("ga_" + n)
    s_init = sem("init")
    s_xT, s_xnT = sem("xT"), sem("xnT")
    s_gates, s_gb, s_gch, s_act = sem("gates"), sem("gate_bias"), sem("gate_chain"), sem("gate_act")
    s_post, s_gF, s_m, s_tr, s_gT, s_m12 = sem("post"), sem("gF"), sem("m"), sem("tr"), sem("gT"), sem("m12")
    s_kT, s_vin = [sem("kT0"), sem("kT1")], [sem("v0"), sem("v1")]
    s_qz, s_v64 = sem("qz"), sem("v64")
    s_qk, s_d, s_dt, s_ct = sem("qk"), sem("d"), sem("dt"), sem("ct")
    s_pv = sem("pv")
    s_oT, s_on = [sem("oT0"), sem("oT1")], [sem("on0"), sem("on1")]
    s_nch, s_d0, s_sq, s_var = sem("norm_chain"), sem("d0"), sem("sq"), sem("var")
    s_pch, s_rr, s_y, s_y2, s_add = sem("pool_chain"), sem("rr"), sem("y"), sem("y2"), sem("add")
    s_zero, s_ssq = sem("zero"), sem("ssq")

    def sync(sp):
        def load(b, par):
            wait(sp, s_qk, (b - 1) * H)
            wait(sp, s_v64, b - 1)
            batch = lambda a: a[b] if isinstance(b, int) else a[bass.ds(b, 1)].rearrange("o r s -> (o r) s")
            sp.dma_start(kT[:, par], batch(c.ins["ctx_T"]).rearrange("(n p) s -> p n s", p=P)).then_inc(s_kT[par], 16)
            sp.dma_start(v_in[:, par], batch(c.ins["ctx_1024"]).rearrange("(t p) d -> p t d", p=P))\
                .then_inc(s_vin[par], 16)
        over_batches(sp, [(0, load)], depth=2)

    def heads(v, n=HD):
        return v.rearrange("p (h d) -> p h d", d=n)

    def tensor(pe):
        wait_weights(pe, w, "ga")

        for b in range(NB):
            pe.wait_ge(ln.s_xn, b + 1)
            wait(pe, s_xnT, b - 1)
            turn_over(pe, ident, ln.xn[:, b % 2], b_turn[b % 2], s_xT)
            lo = WIN - H * b
            wait_once(pe, b, s_zero, 2)
            for n in range(NC):
                pe.matmul(b_gates[:, 0:S], w.gates[:, NC + n, lo:lo + P], c.ctxT[:, n, b * S:(b + 1) * S],
                          start=(b == 0 and n == 0), stop=False, skip_group_check=True)
            pe.wait_ge(s_xnT, b + 1)
            for n in range(NC):
                ins = pe.matmul(b_gates[:, 0:S], w.gates[:, n, lo:lo + P], xnT[:, n, b * S:(b + 1) * S],
                                start=False, stop=(b == NB - 1 and n == NC - 1), skip_group_check=True)
        ins.then_inc(s_gates, 1)
        pe.wait_ge(s_gF, 1)
        pe.matmul(b_post[:, 0:S], c.i_minus_f[:, :], iF[:, :], start=True, stop=True)
        pe.matmul(b_post[:, S:2 * S], c.only_f[:, :], iF[:, :], start=True, stop=True).then_inc(s_post, 1)
        pe.wait_ge(s_act, 3)
        for t in range(NT):
            pe.transpose(b_gates[:, t * G:(t + 1) * G], g[0:G, t * P:(t + 1) * P], ident[0:G, 0:G])
            ins = pe.transpose(b_gates[:, (NT + t) * G:(NT + t + 1) * G], en[0:G, t * P:(t + 1) * P], ident[0:G, 0:G])
        ins.then_inc(s_tr, 1)
        pe.wait_ge(s_gT, 1)
        pe.wait_ge(s_m12, 1)

        def turn_o(b, par):
            for half in range(2):
                pe.wait_ge(s_oT[half], b + 1)
            wait(pe, s_d0, b)
            for t in range(NT):
                for a in range(4):
                    ins = pe.transpose(b_on[t][:, a * P:(a + 1) * P], oT[:, a, t * P:(t + 1) * P], ident[:, :])
                ins.then_inc(s_on[t], 1)

        def scores(b, par, h):
            if h == 0:
                pe.wait_ge(s_kT[par], 16 + 8 * (b - par))
                pe.wait_ge(s_qz, b + 1)
            wait(pe, s_ct, b * H + h - 1)
            bank, n, r = b_qk[h % 2], h // 4, h % 4
            pe.matmul(bank[:, 0:S], kT[:, par, n, 0:P], qz[:, par, r, n, :], start=True, stop=True)
            pe.matmul(bank[:, S:3 * P], kT[:, par, n, P:S], qz[:, par, r, n, P:S], start=True, stop=True)\
                .then_inc(s_qk, 1)

        def decays(b, par, h):
            wait(pe, s_dt, b * H + h - 1)
            bank, row = b_d[h % 2], b * H + h
            one_row = (c.both_halves[:, row:row + 1] if isinstance(b, int) else c.both_halves[:, bass.ds(row, 1)])
            one_row = one_row.broadcast_to([P, P])
            pe.matmul(bank[:, 0:3 * P], one_row, m12[:, :], start=True, stop=False, skip_group_check=True)
            pe.matmul(bank[:, 0:3 * P], one_row, m3[:, :], start=False, stop=False, skip_group_check=True)
            diagonal = bank[:, :].rearrange("p (a b) -> p a b", b=P)[:, 0:3:2, :]
            pe.matmul(diagonal, ident_bf[:, :], c.masked[:, :, :], start=False, stop=True,
                      skip_group_check=True).then_inc(s_d, 1)

        def values(b, par, pair):
            if pair == 0:
                pe.wait_ge(s_v64, b + 1)
            if pair % 2 == 0:
                wait(pe, s_oT[pair // 2], b)
            pe.wait_ge(s_ct, b * H + 2 * pair + 2)
            bank, col = b_o[pair // 2], pair % 2 * S
            for k in range(NT):
                for j in range(2):
                    h = 2 * pair + j
                    p = ct[:, h % CT_RING, :]
                    ins = pe.matmul(bank[VW * j:VW * (j + 1), col + k * P:col + S], v64[:, par, k, h, :],
                                    p[:, 0:S] if k == 0 else p[:, S:3 * P], start=(k == 0), stop=(k == NT - 1),
                                    skip_group_check=True)
            ins.then_inc(s_pv, 1)

        def attend(heads):
            def phase(b, par):
                for h in heads:
                    decays(b, par, h)
                    scores(b, par, h)
                    if h % 2 == 0 and h >= 2:
                        values(b, par, h // 2 - 1)
            return phase

        pe.wait_ge(s_init, 2)
        over_batches(pe, [(0, attend([0])), (1, lambda b, par: values(b, par, 3)), (0, attend([1])), (1, turn_o),
                          (0, attend(range(2, H)))], depth=4)

    def scalar(act):
        wait_weights(act, w, "ga")

        def copy_x(b, par):
            act.wait_ge(s_xT, b + 1)
            xs = xnT[:, :, b * S:(b + 1) * S] if isinstance(b, int) else xnT[:, :, bass.ds(b * S, S)]
            act.activation(xs, b_turn[par][:, :].rearrange("p (n s) -> p n s", n=NC), ACT.Copy).then_inc(s_xnT, 1)

        over_batches(act, [(0, copy_x)], depth=2)
        act.wait_ge(s_gb, 3)
        act.activation(e[G:P, :], neg[G:P, :], ACT.Exp).then_inc(s_act, 1)
        act.wait_ge(s_act, 1)
        act.activation(lsig[G:P, :], e[G:P, :], ACT.Ln, bias=1.0).then_inc(s_act, 1)
        act.wait_ge(s_m, 1)
        act.activation(en[:, :], fm[:, :], ACT.Exp, scale=-1.0).then_inc(s_act, 1)
        act.wait_ge(s_gT, 1)

        def decays(b, par, h):
            act.wait_ge(s_d, b * H + h + 1)
            wait(act, s_ct, b * H + h + 1 - DT_RING)
            bank, row = b_d[h % 2], b * H + h
            slot = dt[:, h % DT_RING, :]
            for k, cols in enumerate((slice(0, S), slice(S, 3 * P))):
                bias = gT[:, k, row:row + 1] if isinstance(b, int) else gT[:, k, bass.ds(row, 1)]
                ins = act.activation(slot[:, cols], bank[:, cols], ACT.Exp, bias=bias)
            ins.then_inc(s_dt, 1)

        def copy_o(b, half):
            act.wait_ge(s_pv, b * 4 + 2 * half + 2)
            wait(act, s_on[1], b)
            act.activation(oT[:, 2 * half:2 * half + 2, :], b_o[half][:, :].rearrange("p (a s) -> p a s", a=2),
                           ACT.Copy).then_inc(s_oT[half], 1)

        def attend(heads):
            def phase(b, par):
                for h in heads:
                    decays(b, par, h)
                    if h == 6:
                        copy_o(b, 0)
            return phase

        def squares(b, par):
            act.wait_ge(s_d0, b + 1)
            wait(act, s_var, b)
            act.activation(sq[:, :, :], d[:, :, :], ACT.Square).then_inc(s_sq, 1)

        over_batches(act, [(0, attend([0])), (1, lambda b, par: copy_o(b, 1)), (0, attend([1, 2, 3])), (1, squares),
                           (0, attend(range(4, H)))], depth=4)

    def vector(dve):
        wait_weights(dve, w, "ga")
        norm_x = ln.vector(dve, x, s_xT)
        for k in range(2):
            col = WIN + k * G
            part = w.gates[:, NC:2 * NC, col:col + H]
            dve.tensor_tensor(part, part, w.gates_v[:, :, k, :], ALU.add).then_inc(s_zero, 1)
        dve.memset(zeros[:, :], 0.0).then_inc(s_zero, 1)
        dve.memset(m3[:, :], 0.0).then_inc(s_zero, 1)
        dve.wait_ge(s_zero, 4)

        def norm(b, par):
            wait_x(dve, w, b)
            norm_x(b, par)

        over_batches(dve, [(0, norm)], depth=2)

        f_rows, ch = slice(G, P), Chain(dve, s_gch, 7)
        ch.start(0)
        dve.wait_ge(s_gates, 1)
        dve.tensor_scalar(iF[0:G, :], b_gates[0:G, 0:S], w.gate_b[0:G, :], None, ALU.add).then_inc(s_gb, 1)
        dve.tensor_scalar(gb[f_rows, :], b_gates[f_rows, 0:S], w.gate_b[f_rows, :], None, ALU.add).then_inc(s_gb, 1)
        dve.wait_ge(s_gb, 2)
        dve.scalar_tensor_tensor(out=neg[f_rows, :], in0=gb[f_rows, :], scalar=-1.0, in1=gb[f_rows, :],
                                 op0=ALU.mult, op1=ALU.min).then_inc(s_gb, 1)
        dve.wait_ge(s_act, 2)
        ch.link(dve.scalar_tensor_tensor(out=lf[f_rows, :], in0=gb[f_rows, :], scalar=0.0, in1=lsig[f_rows, :],
                                         op0=ALU.min, op1=ALU.subtract))
        dve.tensor_tensor_scan(iF[f_rows, :], lf[f_rows, :], zeros[f_rows, :], 0.0, ALU.add, ALU.add).then_inc(s_gF, 1)
        dve.wait_ge(s_post, 1)
        ch.link(dve.tensor_copy(g[:, :], b_post[:, 0:S]))
        ch.link(dve.tensor_tensor_scan(M[:, :], g[:, :], g[:, :], NEG, ALU.max, ALU.max))
        dve.tensor_tensor(fm[:, :], b_post[:, S:2 * S], M[:, :], ALU.add).then_inc(s_m, 1)
        ch.link(dve.tensor_scalar(n1[:, :], M[:, :], -1.0, None, ALU.mult))
        ch.link(dve.scalar_tensor_tensor(out=m_res[:, :], in0=M[:, :], scalar=-1.0, in1=n1[:, :], op0=ALU.mult,
                                         op1=ALU.subtract))
        ch.link(dve.tensor_copy(n2[:, :], m_res[:, :]))
        ch.link(dve.tensor_tensor(n3[:, :], m_res[:, :], n2[:, :], ALU.subtract))
        for dst, src, rows in ((m12, n1, slice(0, G)), (m12, n2, slice(G, P)), (m3, n3, slice(0, G))):
            dve.tensor_copy(dst[rows, 0:S], src[rows, :])
            last = dve.tensor_copy(dst[rows, S:3 * P], src[rows, P:S])
        last.then_inc(s_m12, 1)
        ch.end()
        dve.wait_ge(s_tr, 1)
        dve.tensor_copy(gT[:, :, :], b_gates[:, 0:NT * G].rearrange("p (t g) -> p t g", t=NT))
        dve.tensor_copy(enT[:, :, :], b_gates[:, NT * G:2 * NT * G].rearrange("p (t g) -> p t g", t=NT))\
            .then_inc(s_gT, 1)
        dve.wait_ge(s_gT, 1)

        dve.wait_ge(s_init, 2)

        def spread(b, par):
            wait(dve, s_qk, (b - 1) * H)
            for r in range(4):
                rows = slice(r * HD, (r + 1) * HD)
                src = xnT[rows, :, b * S:(b + 1) * S] if isinstance(b, int) else xnT[rows, :, bass.ds(b * S, S)]
                ins = dve.tensor_copy(qz[rows, par, r], src)
            ins.then_inc(s_qz, 1)

        def decayed(heads):
            def phase(b, par):
                for h in heads:
                    dve.wait_ge(s_qk, b * H + h + 1)
                    dve.wait_ge(s_dt, b * H + h + 1)
                    wait(dve, s_pv, b * 4 + h // 2 - 1)
                    dve.scalar_tensor_tensor(out=ct[:, h % CT_RING, :], in0=b_qk[h % 2][:, 0:3 * P], scalar=SCALE,
                                             in1=dt[:, h % DT_RING, :], op0=ALU.mult, op1=ALU.mult).then_inc(s_ct, 1)
            return phase

        n_ch = Chain(dve, s_nch, 10)

        def centre(b, par):
            n_ch.start(b)
            rows = slice(b * H, (b + 1) * H) if isinstance(b, int) else bass.ds(b * H, H)
            for t in range(NT):
                dve.wait_ge(s_on[t], b + 1)
                on = heads(b_on[t][:, :], VW)
                n_ch.mark(dve.tensor_reduce(mean[:, t, :], on[:, :, 0:HD], AX.X, ALU.add))
                last = n_ch.mark(dve.tensor_copy(total[:, t, :], on[:, :, HD]))
            dve.wait_ge(s_nch, last)
            n_ch.mark(dve.tensor_scalar(mean[:, :, :], mean[:, :, :], 1.0 / HD, None, ALU.mult))
            wait(dve, s_rr, b)
            n_ch.link(dve.scalar_tensor_tensor(out=rn[:, :, :], in0=total[:, :, :], scalar=-1.0,
                                               in1=total[:, :, :], op0=ALU.mult, op1=ALU.max))
            wait(dve, s_sq, b)
            for t in range(NT):
                ins = dve.tensor_tensor(heads(d[:, t, :]), heads(b_on[t][:, :], VW)[:, :, 0:HD],
                                        mean[:, t, :].unsqueeze(2).broadcast_to([P, H, HD]), ALU.subtract)
            ins.then_inc(s_d0, 1)
            n_ch.link(dve.tensor_tensor(rn[:, :, :], rn[:, :, :], enT[:, :, rows], ALU.max))
            n_ch.link(dve.tensor_scalar(rn[:, :, :], rn[:, :, :], EPS, None, ALU.add))
            n_ch.link(dve.reciprocal(rn[:, :, :], rn[:, :, :]))
            n_ch.link(dve.tensor_tensor(r2[:, :, :], rn[:, :, :], rn[:, :, :], ALU.mult))
            n_ch.end()

        def variance(b, par):
            dve.wait_ge(s_sq, b + 1)
            dve.tensor_reduce(ssq[:, :, :], sq[:, :, :].rearrange("p t (h d) -> p t h d", d=HD), AX.X,
                              ALU.add).then_inc(s_ssq, 1)
            dve.wait_ge(s_ssq, b + 1)
            dve.scalar_tensor_tensor(out=var[:, :, :], in0=ssq[:, :, :], scalar=1.0 / HD, in1=r2[:, :, :],
                                     op0=ALU.mult, op1=ALU.mult).then_inc(s_var, 1)
            if isinstance(b, int) and b == NB - 2:
                norm_ahead(c, dve, x, (s_add, AHEAD), parts=(0,))()

        def finish(b, par):
            dve.wait_ge(s_rr, b + 1)
            for t in range(NT):
                ins = dve.tensor_tensor(heads(y[:, t, :]), heads(d[:, t, :]),
                                        rr[:, t, :].unsqueeze(2).broadcast_to([P, H, HD]), ALU.mult)
            ins.then_inc(s_y, 1)
            dve.wait_ge(s_y, b + 1)
            dve.tensor_tensor(z[:, :, :], y[:, :, :], w.norm_w[:, :].unsqueeze(1).broadcast_to([P, NT, D]),
                              ALU.mult).then_inc(s_y2, 1)
            dve.wait_ge(s_y2, b + 1)
            xb = batch_of(x, b)
            dve.tensor_tensor(xb, xb, z[:, :, :], ALU.add).then_inc(s_add, 1)

        over_batches(dve, [(1, decayed([0, 1])), (2, centre), (1, decayed([2, 3])), (2, variance), (0, spread),
                           (1, decayed(range(4, H))), (2, finish)], depth=4,
                     before_last=norm_ahead(c, dve, x, (s_add, AHEAD), parts=(1,)))

    def gpsimd(pool):
        wait_weights(pool, w, "ga")
        norm = ln.gpsimd(pool)
        pool.memset(v64[:, :, :, :, HD:VW], 0.0).then_inc(s_init0, 1)
        pool.wait_ge(s_init0, 1)
        pool.memset(v64[:, :, :, :, HD:HD + 1], 1.0).then_inc(s_init, 1)
        over_batches(pool, [(0, norm)], depth=2)
        pool.memset(qz[:, :], 0.0).then_inc(s_init, 1)

        def spread_v(b, par):
            pool.wait_ge(s_vin[par], 16 + 8 * (b - par))
            wait(pool, s_pv, 4 * (b - 1))
            c.alone(pool)
            for t in range(NT):
                ins = pool.tensor_copy(v64[:, par, t, :, 0:HD], heads(v_in[:, par, t, :]))
            ins.then_inc(s_v64, 1)

        def deviation(b, par):
            pool.wait_ge(s_var, b + 1)
            c.alone(pool)
            pool.tensor_scalar(var2[:, :, :], var[:, :, :], LN_EPS, None, ALU.add).then_inc(s_pch, 1)
            pool.wait_ge(s_pch, b * 2 + 1)
            pool.tensor_tensor(rr[:, :, :], var2[:, :, :], c.minus_half[:, 0:NT * H].rearrange("p (t h) -> p t h", t=NT),
                               ALU.pow).then_inc(s_pch, 1)
            pool.wait_ge(s_pch, b * 2 + 2)
            pool.tensor_tensor(rr[:, :, :], rr[:, :, :], rn[:, :, :], ALU.mult).then_inc(s_rr, 1)
        over_batches(pool, [(0, spread_v), (2, deviation)], depth=4, before_last=norm_ahead(c, pool, x))

    s_init0 = sem("init0")
    return {"norm": ln, "sync": sync, "tensor": tensor, "scalar": scalar, "vector": vector, "gpsimd": gpsimd}


E, FF = 14, 512
NFF = FF // P
LATE = 4
GROUPS = 4
ROW = D + 2
TILES = (2 * NB * S - E) // P + E


def experts(c, x, w):
    banks, ident, early, work = c.banks, c.ident, c.early, c.work
    N_TOK = NB * S
    c.new_stage()
    work.take([P, WORK_WORDS - 2 * E * 2 * FF - 2])
    small = work.used
    w2 = c.take([P, E, NFF, D])
    w1 = c.take([P, E, NC, FF])
    xs = c.nc.dram_tensor("slots", (TILES * P, ROW), F32, kind="Internal").ap()
    ys = c.nc.dram_tensor("results", (2 * N_TOK + P, D), F32, kind="Internal").ap()
    work.used -= (E - LATE) * NC * FF + ROW
    pad = c.take([P, ROW])

    work.used = 0
    ln = LayerNorm(c, "moe")

    def place_small():
        early.clear()
        b = Weights()
        b.xn = early.take([P, TT, ROW])
        b.gate = early.take([P, NC, P])
        b.b1T, b.b2 = early.take([P, E, NFF]), early.take([E, D])
        b.xnT = early.take([P, 2, NC, S])
        b.wT = early.take([E, N_TOK])
        b.w1s = early.take([P, 2, NC, FF])
        b.rows = early.take([P, 2, ROW])
        b.xsT = early.take([P, 2, NC, P])
        b.hT = work.take([P, 2, NFF, P])
        b.res = work.take([P, 2, D])
        b.meta = work.take([P, TILES + 1, 2])
        b.dest = work.take([P, 2, 1], I32)
        return b

    b_ = place_small()
    L, ex, pr, eq1, one1, eq2, one2, mix = [early.take([P, TT, E]) for _ in range(8)]
    L2, slotv = [work.take([P, TT, E]) for _ in range(2)]
    picks_bf = work.take([P, TT, E], BF16)
    col = lambda n=TT: work.take([P, n])
    mx, sm, rs, m1, k1, m2, k2, ws, rw = [col() for _ in range(9)]
    wt = [col(), col()]
    slot_f = [col(), col()]
    slot = [work.take([P, TT], I32) for _ in range(2)]
    place = [work.take([P, TT], I32) for _ in range(2)]
    count_i, count_f = work.take([P, 48], I32), col(48)
    desc, by_tile, before = col(E), col(TT), work.take([P, E, E])
    n_e, t_e, first = col(E), col(E), col(E)
    full = work.take([P, E, TT])
    below = work.take([P, E, E])
    starts = work.take([1, 48, E])
    exp_f, exp_i = work.take([1, 48]), work.take([1, 48], I32)
    tri_bf, ones_bf = work.take([P, P], BF16), work.take([P, P], BF16)
    assert work.used <= small, (work.used, small)

    sem = lambda n: c.sem("moe_" + n)
    s_iota, s_zero, s_small = sem("iota"), sem("zero"), sem("small")
    s_w, s_pad, s_pads = [c.lasting_sem("moe_" + n) for n in ("weights", "pad", "pads_stored")]
    s_xT, s_xnT, s_logit, s_L = sem("xT"), sem("xnT"), sem("logit"), sem("L")
    s_r, s_ex, s_picks, s_mix, s_rank, s_slots, s_wT, s_wTs, s_b2, s_xb = (
        sem("route_chain"), sem("exp"), sem("picks"), sem("mix"), sem("rank"), sem("slots"), sem("wT"),
        sem("wT_sb"), sem("b2"), sem("xn_b2"))
    s_col, s_sc = sem("columns"), [[sem(f"first_choices{g}") for g in range(GROUPS)], [sem("second_choices")]]
    s_rows = [sem("rows0"), sem("rows1")]
    s_T, s_meta, s_xsT, s_w1s, s_h, s_g, s_o, s_res = [sem(n) for n in ("T", "meta", "xsT", "w1s", "h", "g", "o", "res")]
    s_back = [sem("back0"), sem("back1")]
    s_kept, s_xp, s_both = sem("b2_kept"), sem("xn_b2_by_gpsimd"), sem("both_choices")
    s_load = [sem(f"results_loaded{b}") for b in range(NB)]
    s_ch, s_fin = sem("finish_chain"), sem("finished")
    s_exp = sem("expert_table")

    earlier = lambda j, par: j * 8 - 8 * par
    wide = lambda v: v.rearrange("p a b -> p (a b)")
    tw = lambda v: v.unsqueeze(2).broadcast_to([P, TT, E])
    ew = lambda v: v.unsqueeze(1).broadcast_to([P, TT, E])

    def early_gpsimd(pool):
        pool.memset(pad[:, :], 0.0).then_inc(s_pad, 1)
        pool.wait_ge(s_pad, 1)
        pool.iota(pad[:, D:D + 1].bitcast(I32), pattern=[[0, 1]], base=2 * N_TOK, channel_multiplier=1).then_inc(s_pad, 1)

    def early_sync(sp):
        sp.dma_start(w1[:, LATE:], c.ins["L1_ffn_w1"][LATE:].rearrange("e (k p) f -> p e k f", p=P)).then_inc(s_w, 16)
        sp.wait_ge(s_pad, 2)
        sp.dma_start(xs.rearrange("(t p) d -> p t d", p=P), pad[:, :].unsqueeze(1).broadcast_to([P, TILES, ROW])).then_inc(s_pads, 16)

    def sync(sp):
        sp.wait_ge(s_zero, 1)
        sp.dma_start(b_.gate[:, :, 0:E], c.ins["L1_ffn_gate_wT"].rearrange("(n p) e -> p n e", p=P)).then_inc(s_small, 16)
        sp.dma_start(b_.b1T[:, :, :], c.ins["L1_ffn_b1"].rearrange("p (e f) -> p e f", e=E)).then_inc(s_small, 16)
        sp.dma_start(b_.b2[:, :], c.ins["L1_ffn_b2"]).then_inc(s_small, 16)
        sp.wait_ge(s_pads, 16)
        sp.dma_start(w1[:, 0:LATE], c.ins["L1_ffn_w1"][0:LATE].rearrange("e (k p) f -> p e k f", p=P)).then_inc(s_w, 16)
        for e0, e1 in ((0, E // 2), (E // 2, E)):
            sp.dma_start(w2[:, e0:e1], c.ins["L1_ffn_w2"][e0:e1].rearrange("e (k p) d -> p e k d", p=P)).then_inc(s_w, 16)
        for g in range(GROUPS):
            sp.wait_ge(s_sc[0][g], 16 * TT // GROUPS)
        sp.wait_ge(s_sc[1][0], 16 * TT)

        def rows(j, par):
            wait(sp, s_T, j - 1)
            wait(sp, s_meta, j - 1)
            at = bass.ds(j * P, P) if not isinstance(j, int) else slice(j * P, (j + 1) * P)
            sp.dma_start(b_.rows[:, par, :], xs[at, :]).then_inc(s_rows[par], 16)

        over_batches(sp, [(0, rows)], depth=2, n=TILES)

        sp.wait_ge(s_back[0], 16 * ((TILES + 1) // 2))
        sp.wait_ge(s_back[1], 16 * (TILES // 2))
        for b in range(NB):
            for k in range(2):
                sp.dma_start(back[:, k, b * NT:(b + 1) * NT],
                             ys[k * N_TOK + b * S:k * N_TOK + (b + 1) * S].rearrange("(t p) d -> p t d", p=P)).then_inc(s_load[b], 16)
        for b in range(NB):
            store(sp, b)

    back = w1.rearrange("p e k f -> p (e k f)")[:, 0:2 * TT * D].rearrange("p (k t d) -> p k t d", k=2, t=TT)

    KEPT = 4
    kept = [wide(v[:, par]) for v in (ln.xn, b_.xnT) for par in range(2)]

    def store(sp, b):
        sp.wait_ge(s_fin, b + 1)
        sp.dma_start(c.out.rearrange("b (t p) d -> p b t d", p=P)[:, b], x[:, b * NT:(b + 1) * NT]).then_inc(c.s_out, 16)

    def tensor(pe):
        b_x, b_l = banks[0:2], banks[2:4]

        def turn(b, par):
            pe.wait_ge(ln.s_xn, b + 1)
            wait(pe, s_xnT, b - 1)
            turn_over(pe, ident, ln.xn[:, par], b_x[par], s_xT)

        def logits(b, par):
            wait_once(pe, b, s_small, 48)
            pe.wait_ge(s_xnT, b + 1)
            wait(pe, s_L, b - 1)
            for t in range(NT):
                for n in range(NC):
                    ins = pe.matmul(b_l[par][:, t * P:(t + 1) * P], b_.xnT[:, par, n, t * P:(t + 1) * P], b_.gate[:, n, :],
                                    start=(n == 0), stop=(n == NC - 1))
            ins.then_inc(s_logit, 1)

        over_batches(pe, [(0, turn), (1, logits)], depth=4)

        pe.wait_ge(s_picks, 3)
        rank = banks[4][:, 0:TT * E]
        pe.matmul(rank, tri_bf[:, :], wide(picks_bf), start=True, stop=False, skip_group_check=True)
        for t in range(TT - 1):
            n = TT - 1 - t
            pe.matmul(rank[:, (t + 1) * E:], ones_bf[:, :], picks_bf[:, t:t + 1, :].broadcast_to([P, n, E]),
                      start=False, stop=(t == TT - 2), skip_group_check=True)
        pe.matmul(banks[5][:, 0:TT * E], ones_bf[:, :], wide(picks_bf), start=True, stop=True).then_inc(s_rank, 1)

        pe.wait_ge(s_mix, 1)
        for g in range(4):
            for t in range(4):
                ins = pe.transpose(banks[g][0:E, t * P:(t + 1) * P], mix[:, g * 4 + t, :], ident[:, :])
            ins.then_inc(s_wT, 1)
        for b in range(NB):
            pe.wait_ge(s_wTs, max(b // 2 + 1, min(b + 1, 4)))
            if b == 4:
                pe.wait_ge(s_slots, 1)
            for t in range(NT):
                k = b * NT + t
                ins = pe.matmul(banks[b][:, t * D:(t + 1) * D], b_.wT[:, k * P:(k + 1) * P], b_.b2[:, :],
                                start=True, stop=True)
            ins.then_inc(s_b2, 1)

        pe.wait_ge(s_w, 16)
        b_x, b_h, b_o = banks[0:2], banks[2:4], banks[4:6]

        def turn_rows(j, par):
            pe.wait_ge(s_rows[par], earlier(j, par) + 16)
            wait(pe, s_xsT, j - 1)
            for n in range(NC):
                ins = pe.transpose(b_x[par][:, n * P:(n + 1) * P], b_.rows[:, par, n * P:(n + 1) * P], ident[:, :])
            ins.then_inc(s_T, 1)

        def hidden(j, par):
            pe.wait_ge(s_xsT, j + 1)
            pe.wait_ge(s_w1s, j + 1)
            wait(pe, s_g, j - 1)
            for f in range(NFF):
                for n in range(NC):
                    ins = pe.matmul(b_h[par][:, f * P:(f + 1) * P], b_.w1s[:, par, n, f * P:(f + 1) * P], b_.xsT[:, par, n, :],
                                    start=(n == 0), stop=(n == NC - 1))
            ins.then_inc(s_h, 1)

        def output(j, par):
            e = expert_of(pe, j)
            pe.wait_ge(s_g, j + 1)
            if isinstance(j, int) and j < 2:
                pe.wait_ge(s_xb, j + 1)
            wait(pe, s_res, j - 1)
            for f in range(NFF):
                ins = pe.matmul(b_o[par][:, 0:D], b_.hT[:, par, f, :], w2[:, bass.ds(e, 1), f, :].rearrange("p a d -> p (a d)"),
                                start=(f == 0), stop=(f == NFF - 1))
            ins.then_inc(s_o, 1)

        pe.wait_ge(s_exp, 1)
        pe.wait_ge(s_kept, KEPT)
        pe.wait_ge(s_w, 64)
        over_batches(pe, [(0, turn_rows), (1, hidden), (2, output)], depth=4, n=TILES)

    def expert_of(eng, j):
        at = bass.ds(j, 1) if not isinstance(j, int) else slice(j, j + 1)
        return eng.value_load(exp_i[0:1, at], min_val=0, max_val=E - 1)

    def scalar(act):
        def copies(b, par):
            act.wait_ge(ln.s_xn, b + 1)
            act.activation(batch_of(b_.xn, b)[:, :, 0:D], ln.xn[:, par], ACT.Copy)
            act.wait_ge(s_xT, b + 1)
            wait(act, s_logit, b - 1)
            act.activation(wide(b_.xnT[:, par]), banks[par][:, :], ACT.Copy).then_inc(s_xnT, 1)

        over_batches(act, [(0, copies)], depth=2)
        act.wait_ge(s_r, 2)
        act.activation(wide(ex), wide(L2), ACT.Exp).then_inc(s_ex, 1)
        for g in range(4):
            act.wait_ge(s_wT, g + 1)
            act.activation(b_.wT[:, g * 512:(g + 1) * 512], banks[g][0:E, :], ACT.Copy).then_inc(s_wTs, 1)
        act.wait_ge(s_L, NB)
        for b in range(KEPT):
            act.wait_ge(s_b2, b + 1)
            act.activation(kept[b], banks[b][:, :], ACT.Copy).then_inc(s_kept, 1)
        act.wait_ge(s_exp, 1)

        def gelu(j, par):
            e = expert_of(act, j)
            act.wait_ge(s_h, j + 1)
            wait(act, s_o, j - 1)
            for f in range(NFF):
                ins = act.activation(b_.hT[:, par, f, :], banks[2 + par][:, f * P:(f + 1) * P], ACT.Gelu,
                                     bias=b_.b1T[:, bass.ds(e, 1), f])
            ins.then_inc(s_g, 1)

        over_batches(act, [(0, gelu)], depth=2, n=TILES)

    def vector(dve):
        dve.memset(b_.gate[:, :, :], 0.0).then_inc(s_zero, 1)
        statistics, normalise = ln.statistics(dve, x), ln.normalise(dve, x, s_xnT)

        def keep_logits(b, par):
            dve.wait_ge(s_logit, b + 1)
            dve.tensor_copy(batch_of(L, b), banks[2 + par][:, 0:NT * P].rearrange("p (t e) -> p t e", t=NT)[:, :, 0:E]).then_inc(s_L, 1)

        over_batches(dve, [(0, statistics), (1, normalise), (3, keep_logits)], depth=4)

        count = [0]

        def link(ins):
            count[0] += 1
            ins.then_inc(s_r, 1)
            dve.wait_ge(s_r, count[0])

        dve.wait_ge(s_L, NB)
        link(dve.tensor_reduce(mx[:, :], L[:, :, :], AX.X, ALU.max))
        link(dve.tensor_tensor(L2[:, :, :], L[:, :, :], tw(mx), ALU.subtract))
        dve.wait_ge(s_iota, 3)
        dve.tensor_copy(count_f[:, :], count_i[:, :])
        link(dve.tensor_copy(tri_bf[:, :], c.causal_T[:, 0:P]))
        dve.tensor_scalar(desc[:, :], count_f[:, 0:E], -1.0, float(E), ALU.mult, ALU.add)
        dve.tensor_scalar(by_tile[:, :], count_f[:, 0:TT], float(P), None, ALU.mult)
        dve.tensor_copy(ones_bf[:, :], c.ones[:, :]).then_inc(s_picks, 1)
        link(dve.tensor_tensor(before[:, :, :], count_f[:, 0:E].unsqueeze(1).broadcast_to([P, E, E]),
                               count_f[:, 0:E].unsqueeze(2).broadcast_to([P, E, E]), ALU.is_lt))
        dve.wait_ge(s_ex, 1)
        link(dve.tensor_reduce(sm[:, :], ex[:, :, :], AX.X, ALU.add))
        link(dve.reciprocal(rs[:, :], sm[:, :]))
        link(dve.tensor_tensor(pr[:, :, :], ex[:, :, :], tw(rs), ALU.mult))
        link(dve.tensor_reduce(m1[:, :], pr[:, :, :], AX.X, ALU.max))
        link(dve.tensor_tensor(eq1[:, :, :], pr[:, :, :], tw(m1), ALU.is_equal))
        link(dve.tensor_tensor(eq1[:, :, :], eq1[:, :, :], ew(desc), ALU.mult))
        link(dve.tensor_reduce(k1[:, :], eq1[:, :, :], AX.X, ALU.max))
        link(dve.tensor_tensor(one1[:, :, :], eq1[:, :, :], tw(k1), ALU.is_equal))
        link(dve.scalar_tensor_tensor(out=wide(pr), in0=wide(one1), scalar=-2.0, in1=wide(pr), op0=ALU.mult, op1=ALU.add))
        link(dve.tensor_reduce(m2[:, :], pr[:, :, :], AX.X, ALU.max))
        link(dve.tensor_tensor(eq2[:, :, :], pr[:, :, :], tw(m2), ALU.is_equal))
        link(dve.tensor_tensor(eq2[:, :, :], eq2[:, :, :], ew(desc), ALU.mult))
        link(dve.tensor_reduce(k2[:, :], eq2[:, :, :], AX.X, ALU.max))
        link(dve.tensor_tensor(one2[:, :, :], eq2[:, :, :], tw(k2), ALU.is_equal))
        link(dve.tensor_tensor(wide(picks_bf), wide(one1), wide(one2), ALU.add))
        dve.tensor_tensor(ws[:, :], m1[:, :], m2[:, :], ALU.add).then_inc(s_picks, 2)
        dve.wait_ge(s_picks, 3)
        link(dve.tensor_scalar(ws[:, :], ws[:, :], 1e-10, None, ALU.max))
        link(dve.reciprocal(rw[:, :], ws[:, :]))
        dve.tensor_tensor(wt[0], m1[:, :], rw[:, :], ALU.mult)
        link(dve.tensor_tensor(wt[1], m2[:, :], rw[:, :], ALU.mult))
        dve.tensor_tensor(eq1[:, :, :], one1[:, :, :], tw(wt[0]), ALU.mult)
        link(dve.tensor_tensor(eq2[:, :, :], one2[:, :, :], tw(wt[1]), ALU.mult))
        dve.tensor_tensor(wide(mix), wide(eq1), wide(eq2), ALU.add).then_inc(s_mix, 1)
        dve.wait_ge(s_rank, 1)
        link(dve.tensor_reduce(n_e[:, :], banks[5][:, 0:TT * E].rearrange("p (t e) -> p e t", t=TT), AX.X, ALU.add))
        link(dve.tensor_tensor(full[:, :, :], n_e[:, :].unsqueeze(2).broadcast_to([P, E, TT]),
                               by_tile[:, :].unsqueeze(1).broadcast_to([P, E, TT]), ALU.is_gt))
        link(dve.tensor_reduce(t_e[:, :], full[:, :, :], AX.X, ALU.add))
        link(dve.tensor_tensor(below[:, :, :], before[:, :, :], t_e[:, :].unsqueeze(1).broadcast_to([P, E, E]), ALU.mult))
        link(dve.tensor_reduce(first[:, :], below[:, :, :], AX.X, ALU.add))
        link(dve.scalar_tensor_tensor(out=slotv[:, :, :], in0=ew(first), scalar=float(P),
                                      in1=banks[4][:, 0:TT * E].rearrange("p (t e) -> p t e", t=TT), op0=ALU.mult, op1=ALU.add))
        dve.tensor_tensor(eq1[:, :, :], slotv[:, :, :], one1[:, :, :], ALU.mult)
        link(dve.tensor_tensor(eq2[:, :, :], slotv[:, :, :], one2[:, :, :], ALU.mult))
        dve.tensor_reduce(slot_f[0], eq1[:, :, :], AX.X, ALU.add)
        link(dve.tensor_reduce(slot_f[1], eq2[:, :, :], AX.X, ALU.add))
        for k in range(2):
            ins = dve.tensor_scalar(slot[k], slot_f[k], -1.0, None, ALU.add)
        ins.then_inc(s_slots, 1)
        columns(dve, 0, slice(0, TT))
        link(dve.tensor_tensor(starts[:, :, :], first[0:1, :].unsqueeze(1).broadcast_to([1, 48, E]),
                               count_f[0:1, :].unsqueeze(2).broadcast_to([1, 48, E]), ALU.is_le))
        link(dve.tensor_reduce(exp_f[:, :], starts[:, :, :], AX.X, ALU.add))
        dve.tensor_scalar(exp_i[:, :], exp_f[:, :], -1.0, None, ALU.add).then_inc(s_exp, 1)
        for g in range(GROUPS):
            dve.wait_ge(s_sc[0][g], 16 * TT // GROUPS)
            columns(dve, 1, slice(g * TT // GROUPS, (g + 1) * TT // GROUPS))
        dve.wait_ge(s_sc[1][0], 16 * TT)
        dve.wait_ge(s_exp, 1)

        def add_b2(b):
            dve.wait_ge(s_b2, b + 1)
            xb = b_.xn[:, b * NT:(b + 1) * NT, 0:D]
            dve.tensor_tensor(xb, banks[b][:, :].rearrange("p (t d) -> p t d", t=NT), xb, ALU.add).then_inc(s_xb, 1)

        def take_rows(j, par):
            dve.wait_ge(s_rows[par], earlier(j, par) + 16)
            at = bass.ds(j, 1) if not isinstance(j, int) else slice(j, j + 1)
            dve.tensor_copy(b_.meta[:, at, :], b_.rows[:, par, D:ROW].unsqueeze(1)).then_inc(s_meta, 1)
            e = expert_of(dve, j)
            wait(dve, s_h, j - 1)
            dve.tensor_copy(b_.w1s[:, par].unsqueeze(1), w1[:, bass.ds(e, 1)]).then_inc(s_w1s, 1)
            dve.wait_ge(s_T, j + 1)
            dve.tensor_copy(wide(b_.xsT[:, par]), banks[par][:, 0:S]).then_inc(s_xsT, 1)
            if isinstance(j, int) and j < 2:
                for b in range(KEPT + 2 * j, KEPT + 2 * j + 2):
                    add_b2(b)

        def results(j, par):
            at = bass.ds(j, 1) if not isinstance(j, int) else slice(j, j + 1)
            dve.wait_ge(s_o, j + 1)
            dve.wait_ge(s_meta, at_most(j + 3, TILES) if isinstance(j, int) else j + 3)
            wait(dve, s_back[par], earlier(j, par))
            dve.tensor_copy(b_.dest[:, par], b_.meta[:, at, 0].bitcast(I32))
            dve.tensor_scalar(b_.res[:, par], banks[4 + par][:, 0:D], b_.meta[:, at, 1], None, ALU.mult).then_inc(s_res, 1)

        dve.wait_ge(s_w, 64)
        over_batches(dve, [(0, take_rows), (2, results)], depth=4, n=TILES)

        for b in range(NB):
            dve.wait_ge(s_both, b + 1)
            if b < KEPT:
                dve.wait_ge(s_xp, b + 1)
            xb, f = x[:, b * NT:(b + 1) * NT], back[:, 0, b * NT:(b + 1) * NT]
            dve.tensor_tensor(f, f, b_.xn[:, b * NT:(b + 1) * NT, 0:D], ALU.add).then_inc(s_ch, 1)
            dve.wait_ge(s_ch, 2 * b + 1)
            dve.tensor_scalar(f, f, -100.0, 100.0, ALU.max, ALU.min).then_inc(s_ch, 1)
            dve.wait_ge(s_ch, 2 * b + 2)
            dve.tensor_tensor(xb, f, xb, ALU.add).then_inc(s_fin, 1)

    def columns(dve, k, tiles):
        dve.tensor_copy(b_.xn[:, tiles, D].bitcast(I32), place[k][:, tiles])
        dve.tensor_copy(b_.xn[:, tiles, D + 1], wt[k][:, tiles]).then_inc(s_col, 1)

    def gpsimd(pool):
        pool.iota(count_i[:, :], pattern=[[1, 48]], base=0, channel_multiplier=0).then_inc(s_iota, 1)
        for k in range(2):
            pool.iota(place[k], pattern=[[P, TT]], base=k * N_TOK, channel_multiplier=1).then_inc(s_iota, 1)
        norm = ln.gpsimd(pool)
        over_batches(pool, [(0, norm)], depth=2)
        pool.wait_ge(s_pads, 16)
        pool.wait_ge(s_slots, 1)
        pool.wait_ge(s_xnT, NB)
        for k in range(2):
            for t in range(TT):
                if k == 0 and t == 0:
                    pool.wait_ge(s_col, 1)
                if k == 1 and t % (TT // GROUPS) == 0:
                    pool.wait_ge(s_col, 2 + t // (TT // GROUPS))
                pool.indirect_dma_start(xs, bass.IndirectOffsetOnAxis(ap=slot[k][:, t:t + 1], axis=0),
                                        b_.xn[:, t, :], None).then_inc(s_sc[0][t // (TT // GROUPS)] if k == 0 else s_sc[1][0], 16)

        pool.wait_ge(s_sc[1][0], 16 * TT)
        for b in range(KEPT):
            pool.wait_ge(s_kept, b + 1)
            xb = b_.xn[:, b * NT:(b + 1) * NT, 0:D]
            pool.tensor_tensor(xb, kept[b].rearrange("p (t d) -> p t d", t=NT), xb, ALU.add).then_inc(s_xp, 1)

        def send(j, par):
            pool.wait_ge(s_res, j + 1)
            c.alone(pool)
            pool.indirect_dma_start(ys, bass.IndirectOffsetOnAxis(ap=b_.dest[:, par], axis=0),
                                    b_.res[:, par], None, bounds_check=2 * N_TOK - 1, oob_is_err=False).then_inc(s_back[par], 16)

        over_batches(pool, [(0, send)], depth=2, n=TILES)

        for b in range(NB):
            pool.wait_ge(s_load[b], 32)
            f, g = [back[:, k, b * NT:(b + 1) * NT] for k in range(2)]
            pool.tensor_tensor(f, f, g, ALU.add).then_inc(s_both, 1)

    return {"norm": ln, "tensor": tensor, "scalar": scalar, "vector": vector, "gpsimd": gpsimd, "sync": sync,
            "early_gpsimd": early_gpsimd, "early_sync": early_sync}


STAGES = [linear_attention, cross_attention, low_rank_ffn, causal_linear_attention,
          gated_attention, experts]
AHEAD = 2
EARLY_AFTER = 2


def build(nc, ins, out, stages=STAGES):
    with ExitStack() as ctx:
        c = Core(nc, ctx)
        c.ins = ins
        x = c.sb("x", [P, TT, D])
        w = Weights()
        programs = [setup(c, x, w, ins)]
        s_end = [c.sem(f"end_of_stage_{k}") for k in range(len(stages) + 1)]
        c.out, c.s_out = out, c.sem("stored")
        stage_sems = []
        held = [ExitStack() for _ in stages]
        for k, stage in enumerate(stages):
            c.stage_sems, c.given = held[k], []
            programs.append(stage(c, x, w))
            stage_sems.append(c.given)
            if k:
                held[k - 1].close()
        held[-1].close()
        for program in programs[2:]:
            program["norm"].ahead = AHEAD
        compute = ("tensor", "scalar", "vector", "gpsimd")

        def run(name, eng):
            for k, program in enumerate(programs):
                if k == min(EARLY_AFTER + 1, len(programs) - 1) and "early_" + name in programs[-1]:
                    programs[-1]["early_" + name](eng)
                c.next_norm = programs[k + 1]["norm"] if 0 < k < len(programs) - 1 else None
                if name in program:
                    program[name](eng)
                if k and (k < len(programs) - 1 or name != "sync"):
                    eng.drain().then_inc(s_end[k], 1)
                if k and k < len(programs) - 1:
                    eng.wait_ge(s_end[k], 5)
                    if name == "gpsimd":
                        for s in stage_sems[k - 1]:
                            eng.sem_clear(s)

        block = ctx.enter_context(nc.Block())

        @block.sync
        def _(sp):
            run("sync", sp)
            sp.wait_ge(c.s_out, 16 * NB)

        @block.tensor
        def _(pe):
            run("tensor", pe)

        @block.scalar
        def _(act):
            run("scalar", act)

        @block.vector
        def _(dve):
            run("vector", dve)

        @block.gpsimd
        def _(pool):
            run("gpsimd", pool)


def laid_out(inputs):
    a = {k: np.ascontiguousarray(np.asarray(v)) for k, v in inputs.items()}
    for name in TURNED:
        a[name + "T"] = np.ascontiguousarray(a.pop(name).T)
    a["ctx_T"] = np.ascontiguousarray(a["ctx_1024"].transpose(0, 2, 1))
    for name in ("L0_xattn_wq", "L0_xattn_wk"):
        by_head = a.pop(name).T.reshape(D, 2, 2, 4, 16)
        a[name + "_h"] = np.ascontiguousarray(by_head.transpose(0, 1, 2, 4, 3).reshape(D, D))
    a["gate_b"] = np.concatenate([np.tile(a.pop("L1_xattn_igate_b"), NB), np.tile(a.pop("L1_xattn_fgate_b"), NB)])[:, None]
    a["L1_ffn_b1"] = np.ascontiguousarray(a["L1_ffn_b1"].reshape(-1, P).T)
    for name in COLUMNS:
        a[name] = np.ascontiguousarray(a[name].reshape(-1, P).T)
    return a


def kernel(**inputs):
    import concourse.bacc as bacc
    from concourse.bass_utils import run_bass_kernel_spmd

    nc = bacc.Bacc("TRN2", target_bir_lowering=False, num_devices=1)
    arrays = laid_out(inputs)
    ins = {k: nc.dram_tensor("in_" + k, a.shape, mybir.dt.from_np(a.dtype), kind="ExternalInput").ap()
           for k, a in arrays.items()}
    out = nc.dram_tensor("out_0", (NB, S, D), F32, kind="ExternalOutput").ap()
    build(nc, ins, out)
    r = run_bass_kernel_spmd(nc, [{"in_" + k: a for k, a in arrays.items()}], core_ids=[0])
    return r.results[0]["out_0"]
```
